# Optimizing a Trainium2 kernel written in Bass

```python
import numpy as np
import jax
import jax.numpy as jnp

def _softmax(x, axis=-1):
    return jax.nn.softmax(x, axis=axis)

def _gelu(x):
    return jax.nn.gelu(x, approximate=True)

def _silu(x):
    return jax.nn.silu(x)

def _sigmoid(x):
    return jax.nn.sigmoid(x)

def _layernorm(x, axis=-1, eps=1e-05):
    m = jnp.mean(x, axis=axis, keepdims=True)
    v = jnp.var(x, axis=axis, keepdims=True)
    return (x - m) / jnp.sqrt(v + eps)

def _scatter_add(tgt, idx, src, axis=0):
    return tgt.at[idx].add(src)

def _segment_sum(src, seg, n):
    return jax.ops.segment_sum(src, seg, n)
kernel_name = 'mk_gnn_resnorm_d2_gnn_r8_408538'

def setup_inputs(seed: int=0):
    np.random.seed(seed)
    _w = jnp.asarray

    def _rec_inputs():
        import jax
        import jax.numpy as jnp
        _gk = jax.random.key(seed)
        x = -0.000202 + 1 * jax.random.normal(jax.random.fold_in(_gk, 1), (12500, 128), jnp.float32)
        src = jax.random.randint(jax.random.fold_in(_gk, 2), (200000,), 0, 12500, jnp.int32)
        dst = jnp.minimum((12500 * jax.random.uniform(jax.random.fold_in(_gk, 3), (200000,)) ** 2.0).astype(jnp.int32), 99999)
        _o = jnp.argsort(dst, stable=True)
        src = src[_o]
        dst = dst[_o]
        return (x, src, dst)
    x, src, dst = _rec_inputs()

    def _L0_gnn_setup():
        import jax, jax.numpy as jnp
        import numpy as np
        N_NODES = 6250
        N_EDGES = 100000
        D = 128
        L = 3
        key = jax.random.key(seed)
        ks = jax.random.split(key, 8)
        h = jax.random.normal(ks[0], (N_NODES, D), dtype=jnp.float32)
        src = jax.random.randint(ks[1], (N_EDGES,), 0, N_NODES, dtype=jnp.int32)
        dst = jax.random.randint(ks[2], (N_EDGES,), 0, N_NODES, dtype=jnp.int32)
        w_scale = 0.05
        W1 = jax.random.normal(ks[3], (L, D, D), dtype=jnp.float32) * w_scale
        b1 = jnp.zeros((L, D), dtype=jnp.float32)
        W2 = jax.random.normal(ks[4], (L, D, D), dtype=jnp.float32) * w_scale
        b2 = jnp.zeros((L, D), dtype=jnp.float32)
        eps = jnp.zeros((L,), dtype=jnp.float32)
        return {'h': h, 'src': src, 'dst': dst, 'W1': W1, 'b1': b1, 'W2': W2, 'b2': b2, 'eps': eps}
    _L0_gnn_all = _L0_gnn_setup()
    _L0_gnn_in = {k: v for k, v in _L0_gnn_all.items() if k in ('W1', 'b1', 'W2', 'b2', 'eps')}
    del _L0_gnn_all

    def _L1_gnn_setup():
        import jax, jax.numpy as jnp
        import numpy as np
        N_NODES = 2500
        N_EDGES = 80000
        CHANNEL = 128
        LEAKY_ALPHA = 0.2
        key = jax.random.key(seed)
        k_h, k_w, k_a, k_s, k_d = jax.random.split(key, 5)
        C = CHANNEL
        h = jax.random.normal(k_h, (N_NODES, C), dtype=jnp.float32)
        w = jax.random.normal(k_w, (2 * C, C), dtype=jnp.float32) * np.sqrt(2.0 / (3 * C))
        a = jax.random.normal(k_a, (C, 1), dtype=jnp.float32) * np.sqrt(2.0 / (C + 1))
        src = jax.random.randint(k_s, (N_EDGES,), 0, N_NODES, dtype=jnp.int32)
        dst = jax.random.randint(k_d, (N_EDGES,), 0, N_NODES, dtype=jnp.int32)
        return {'h': h, 'w': w, 'a': a, 'src': src, 'dst': dst}
    _L1_gnn_all = _L1_gnn_setup()
    _L1_gnn_in = {k: v for k, v in _L1_gnn_all.items() if k in ('w', 'a')}
    del _L1_gnn_all
    return {'x': x, 'src': src, 'dst': dst, 'L0_gnn_W1': _L0_gnn_in['W1'], 'L0_gnn_b1': _L0_gnn_in['b1'], 'L0_gnn_W2': _L0_gnn_in['W2'], 'L0_gnn_b2': _L0_gnn_in['b2'], 'L0_gnn_eps': _L0_gnn_in['eps'], 'L1_gnn_w': _L1_gnn_in['w'], 'L1_gnn_a': _L1_gnn_in['a']}

def reference(x, src, dst, L0_gnn_W1, L0_gnn_b1, L0_gnn_W2, L0_gnn_b2, L0_gnn_eps, L1_gnn_w, L1_gnn_a):
    import jax
    import jax.numpy as jnp

    def _L0_gnn_ref(h, src, dst, W1, b1, W2, b2, eps):
        import jax, jax.numpy as jnp
        import numpy as np
        N_NODES = 6250
        N_EDGES = 100000
        D = 128
        L = 3
        n = h.shape[0]
        for l in range(W1.shape[0]):
            agg = jax.ops.segment_sum(h[src], dst, num_segments=n)
            z = (1.0 + eps[l]) * h + agg
            hid = jnp.maximum(z @ W1[l] + b1[l], 0.0)
            h = hid @ W2[l] + b2[l]
        return h

    def _L1_gnn_ref(h, w, a, src, dst):
        import jax, jax.numpy as jnp
        import numpy as np
        N_NODES = 2500
        N_EDGES = 80000
        CHANNEL = 128
        LEAKY_ALPHA = 0.2
        N = h.shape[0]
        hi = h[src]
        hj = h[dst]
        hij = jnp.concatenate([hi, hj], axis=-1)
        e = jnp.matmul(jax.nn.leaky_relu(jnp.matmul(hij, w), LEAKY_ALPHA), a)
        exp_e = jnp.exp(e)
        denom = jax.ops.segment_sum(exp_e, src, num_segments=N)
        att = exp_e / denom[src]
        out = jax.ops.segment_sum(hi * att, dst, num_segments=N)
        return out
    x = _layernorm(x + _L0_gnn_ref(x, src, dst, L0_gnn_W1, L0_gnn_b1, L0_gnn_W2, L0_gnn_b2, L0_gnn_eps), axis=-1)
    x = _layernorm(x + _L1_gnn_ref(x, L1_gnn_w, L1_gnn_a, src, dst), axis=-1)
    return x

_drawn_inputs = setup_inputs


def setup_inputs(seed=0):
    import zlib

    import numpy as np

    out = dict(_drawn_inputs(seed))
    spreads = {'L0_gnn_b1': (0.0, 0.1), 'L0_gnn_b2': (0.0, 0.1), 'L0_gnn_eps': (0.0, 2.0)}
    factors = {'L1_gnn_w': 4.339, 'L1_gnn_a': 4.181}
    for name, (base, spread) in spreads.items():
        noise = np.random.default_rng([zlib.crc32(name.encode()), seed]).standard_normal(out[name].shape)
        drawn = base * np.exp(spread * noise) if base else spread * noise
        out[name] = jnp.asarray(drawn.astype(out[name].dtype))
    for name, factor in factors.items():
        out[name] = (out[name] * factor).astype(out[name].dtype)
    return out
```

```python
from contextlib import ExitStack

import numpy as np

import concourse.bass as bass
from concourse import mybir
from concourse.alu_op_type import AluOpType as ALU

f32 = mybir.dt.float32
bf16 = mybir.dt.bfloat16
i32 = mybir.dt.int32
i16 = mybir.dt.int16
ACT = mybir.ActivationFunctionType
AX = mybir.AxisListType.X

P = 128
D = 128
N = 12500
E = 200000
LAYERS = 3
W = 512
C = W // P
BLOCKS = -(-N // W)
TAIL = N - (BLOCKS - 1) * W
TAIL_C = TAIL // P
TAIL_R = TAIL - TAIL_C * P
NPAD = BLOCKS * W
PAIR = 2 * P
GPI = 8
TPI = 2 * GPI
HALF = GPI // 2
TURNS = -(-(E // PAIR + BLOCKS) // GPI)
G = TURNS * GPI
RG = -(-G // P)
QPAD = RG * P * PAIR
BANKS = 4
ROW1 = D + 4
SPLIT = 3 * D
AGG0 = 16 * BLOCKS
NEG_SLOPE = 0.2
LN_EPS = 1e-5
EP = 125
EC = E // EP
assert EP * EC == E and RG * P >= G and AGG0 + NPAD == BLOCKS * C * ROW1


class Count:

    def __init__(self, eng, sem):
        self.eng, self.sem, self.base, self.k, self.outer = eng, sem, 0, 0, []

    def add(self, ins):
        ins.then_inc(self.sem, 1)
        self.k += 1

    def wait(self):
        self.eng.wait_ge(self.sem, self.base + self.k)

    def enter(self, turn, per_turn):
        self.outer.append((self.base, self.k, per_turn))
        self.base, self.k = self.base + self.k + turn * per_turn, 0

    def leave(self, turns):
        base, k, per_turn = self.outer.pop()
        assert self.k == per_turn, f"a turn adds {self.k}, not {per_turn}"
        self.base, self.k = base, k + turns * per_turn


def gnn(nc, x, src, dst, w1, b1, w2, b2, eps, w, a, out):
    ctx = ExitStack()
    with ctx:
        def sb(name, shape, dt):
            return ctx.enter_context(nc.sbuf_tensor(name, shape, dt))

        def sem(name):
            return ctx.enter_context(nc.semaphore(name))

        def sems(name, n):
            return [sem(f"{name}{i}") for i in range(n)]

        ds = bass.ds

        edge_src = nc.dram_tensor("edge_src", (QPAD // PAIR, PAIR), i32).ap()
        edge_dst = nc.dram_tensor("edge_dst", (QPAD // PAIR, PAIR), i32).ap()
        block_row = nc.dram_tensor("block_row", (1, RG * P), i32).ap()
        rel_rows = nc.dram_tensor("rel_rows", (RG * P, PAIR), i16).ap()
        table_h = nc.dram_tensor("table_h", (NPAD, SPLIT), bf16).ap()
        table_p = nc.dram_tensor("table_p", (NPAD, ROW1), f32).ap()
        table_x1 = nc.dram_tensor("table_x1", (-(-N // P) * P, ROW1), f32).ap()

        big = sb("big", [P, AGG0 + NPAD], f32)
        agg = big[:, AGG0:AGG0 + NPAD]
        x1_rows = sb("x1_rows", [P, BLOCKS * C, ROW1], f32)
        room = x1_rows[:, :, :].rearrange("p c d -> p (c d)")
        QW = RG * PAIR
        g_src = room[:, 0:QW].bitcast(i32).rearrange("p (r e) -> p r e", r=RG)
        g_dst = room[:, QW:2 * QW].bitcast(i32).rearrange("p (r e) -> p r e", r=RG)
        g_srcf = room[:, 2 * QW:3 * QW].rearrange("p (r e) -> p r e", r=RG)
        g_rel = room[:, 3 * QW:4 * QW].rearrange("p (r e) -> p r e", r=RG)
        g_rel16 = room[:, 4 * QW:4 * QW + QW // 2].bitcast(i16).rearrange("p (r e) -> p r e", r=RG)
        given_src = room[0:EP, 0:EC].bitcast(i32)
        given_dst = room[0:EP, EC:2 * EC + 1].bitcast(i32)
        given_bi = room[0:EP, 2 * EC + 1:3 * EC + 2].bitcast(i32)
        given_b = room[0:EP, 3 * EC + 2:4 * EC + 3]
        given_down = room[0:EP, 4 * EC + 3:5 * EC + 3]
        assert 5 * EC + 3 <= 5 * QW
        PP, PC = 96, 306
        pad_src = room[0:PP, 5 * QW:5 * QW + PC].bitcast(i32)
        pad_dst = room[0:PP, 5 * QW + PC:5 * QW + 2 * PC].bitcast(i32)
        iota_i = room[:, 5 * QW + 2 * PC:5 * QW + 2 * PC + W].bitcast(i32)
        assert PP * PC == QPAD - E and 5 * QW + 2 * PC + W <= BLOCKS * C * ROW1
        src_t = sb("src_t", [P, 2 * G], i32)
        rel_t = sb("rel_t", [P, 2 * G], f32)
        exp_t = sb("exp_t", [P, 2 * G], f32)

        rows = sb("rows", [P, TPI, SPLIT], bf16)
        rows_f = rows[:, :, :].bitcast(f32)
        hot = sb("hot", [P, BANKS, 2 * W * 2], f32)
        hot_bf = hot[:, :, 0:W].bitcast(bf16).rearrange("p s (k w) -> p s k w", k=2)
        hot_w = hot[:, :, 0:2 * W].rearrange("p s (k w) -> p s k w", k=2)
        hot_t = hot[:, :, 0:C * PAIR].rearrange("p s (c e) -> p s c e", c=C)
        between = hot[:, :, :].rearrange("p s w -> p (s w)")
        x_in = between[:, 0:2 * W].rearrange("p (s c d) -> p s c d", s=2, c=C)
        y = between[:, 2 * W:4 * W].rearrange("p (s c d) -> p s c d", s=2, c=C)
        rest = between[:, 4 * W:5 * W].rearrange("p (c d) -> p c d", c=C)
        den_s = between[:, 5 * W:5 * W + 2 * P].rearrange("p (k n) -> p k n", k=2)
        idx_now = sb("idx_now", [P, TPI], i32)
        rel_now = sb("rel_now", [P, TPI], f32)
        exp_now = sb("exp_now", [P, TPI], f32)

        stage = sb("stage", [P, 8 * W + P], f32)
        hid = stage[:, 0:2 * W].rearrange("p (s w) -> p s w", s=2)
        h_t = stage[:, 2 * W:4 * W].rearrange("p (s w) -> p s w", s=2)
        norm = stage[:, 4 * W:6 * W].rearrange("p (s c d) -> p s c d", s=2, c=C)
        x1_t = stage[:, 6 * W:8 * W].rearrange("p (s w) -> p s w", s=2)
        DEN, TW = 8 * 2 * P, BANKS * 2 * ROW1
        den_hot = stage[:, 0:DEN].rearrange("p (s h n) -> p s h n", s=8, h=2)
        pre = stage[:, DEN:DEN + TW].rearrange("p (s k d) -> p s k d", s=BANKS, k=2)
        pos = stage[:, DEN + TW:DEN + TW + BANKS * PAIR].rearrange("p (s k d) -> p s k d", s=BANKS, k=2)
        assert DEN + TW + BANKS * PAIR <= 8 * W + P

        split = sb("split", [P, 2, C, SPLIT], bf16)
        p_rows = sb("p_rows", [P, 2, C, ROW1], f32)
        rel_row = split[:, :, :, :].rearrange("p s c f -> p (s c f)")[:, 0:2 * HALF * PAIR].bitcast(i16) \
            .rearrange("p (h e) -> p h e", h=2)
        stats = sb("stats", [P, C, 6], f32)
        mean_var = sb("mean_var", [P, 2, C, 2], f32)
        std = sb("std", [P, 2, C], f32)
        rstd = sb("rstd", [P, 2, C], f32)

        ident = sb("ident", [P, P], f32)
        ones = sb("ones", [P, P], f32)
        zeros = sb("zeros", [P, P], f32)
        iota16 = sb("iota16", [P, W], i16)
        iota_f = sb("iota_f", [P, W], f32)
        node_i = sb("node_i", [P, C], i32)
        node_c = sb("node_c", [P, C], f32)
        group_i = sb("group_i", [P, RG], i32)
        group_c = sb("group_c", [P, RG], f32)
        first_i = sb("first_i", [P, BLOCKS], i32)
        first_f = sb("first_f", [P, BLOCKS], f32)
        block_f = sb("block_f", [P, BLOCKS], f32)

        before = stage[:, 0:P]
        steps_down = sb("steps_down", [P, 1], f32)
        unordered = sb("unordered", [1, 1], i32)
        place = sb("place", [P, BLOCKS], f32)
        edge_hot = sb("edge_hot", [P, BLOCKS], f32)
        edge_rank = sb("edge_rank", [P, BLOCKS], f32)
        edge_place = sb("edge_place", [P, 1], f32)
        edge_place_i = sb("edge_place_i", [P, 1], i32)
        edge_now = sb("edge_now", [P, 2], i32)
        last_i = sb("last_i", [P, RG], i32)
        last_f = sb("last_f", [P, RG], f32)
        below = sb("below", [P, RG, BLOCKS], f32)
        start = sb("start", [P, BLOCKS], f32)
        group_b = sb("group_b", [P, RG], f32)
        group_b512 = sb("group_b512", [P, RG], f32)
        group_bi = sb("group_bi", [P, RG], i32)
        pair_f = sb("pair_f", [P, RG], f32)
        pair_i = sb("pair_i", [P, RG], i32)
        base_row = sb("base_row", [1, RG * P], i32)

        w1_s = sb("w1_s", [P, D], f32)
        w2_s = sb("w2_s", [P, D], f32)
        b1_s = sb("b1_s", [P, 1], f32)
        b2_s = sb("b2_s", [P, 1], f32)
        w_s = sb("w_s", [P, 2, D], f32)
        wa_s = sb("wa_s", [P, 2], f32)
        a_row = sb("a_row", [P, D], f32)
        a_08 = sb("a_08", [P, D], f32)
        junk = stage[:, P:P + D]
        eps1 = sb("eps1", [P, LAYERS], f32)
        ln_eps = sb("ln_eps", [P, 1], f32)
        score = sb("score", [P, TPI], f32)
        inside = sb("inside", [P, TPI], f32)
        rel_turn = sb("rel_turn", [P, TPI], f32)
        outside = sb("outside", [P, TPI], f32)
        masked_s = sb("masked_s", [P, TPI], f32)
        hilo_i = sb("hilo_i", [P, 2, TPI], i32)
        hilo = sb("hilo", [P, 2, TPI], f32)
        att = sb("att", [P, TPI], f32)

        ps = [ctx.enter_context(nc.psum_tensor(f"ps{i}", [P, W], f32)) for i in range(8)]
        den_ps = ps[4][:, 0:P]
        HI = -(-N // P)

        const_in = sem("const_in")
        edges_in = sem("edges_in")
        last_in = sem("last_in")
        base_out = sem("base_out")
        base_in = sem("base_in")
        rel_out = sem("rel_out")
        given_in = sem("given_in")
        down_ready = sem("down_ready")
        down_summed = sem("down_summed")
        order_known = sem("order_known")
        starts_ready = sem("starts_ready")
        starts_summed = sem("starts_summed")
        edge_hot_ready = sem("edge_hot_ready")
        edge_ranked = sem("edge_ranked")
        edge_placed = sem("edge_placed")
        edge_moved = sem("edge_moved")
        regrouped = sem("regrouped")
        consts = sem("consts")
        ones_set = sem("ones_set")
        counted = sem("counted")
        summed_b = sem("summed_b")
        pairs_ready = sem("pairs_ready")
        edges_g = sem("edges_g")
        g_ready = sem("g_ready")
        g_flipped = sem("g_flipped")
        g_taken = sem("g_taken")
        weights_in = sem("weights_in")
        x_loaded = sems("x_loaded", 2)
        x_flipped = sem("x_flipped")
        x_taken = sem("x_taken")
        split_done = sem("split_done")
        table_out = sems("table_out", 2)
        staged = sem("staged")
        row_in = sems("row_in", TPI)
        hot_ready = sem("hot_ready")
        group_summed = sem("group_summed")
        bank_free = sem("bank_free")
        up_done = sem("up_done")
        hid_done = sem("hid_done")
        down_done = sem("down_done")
        h_done = sem("h_done")
        agg_set = sem("agg_set")
        h_flipped = sem("h_flipped")
        var_ready = sem("var_ready")
        std_ready = sem("std_ready")
        norm_done = sem("norm_done")
        x1_kept = sem("x1_kept")
        x1_flipped = sem("x1_flipped")
        x1_t_done = sem("x1_t_done")
        pq_done = sem("pq_done")
        p_taken = sem("p_taken")
        q_taken = sem("q_taken")
        p_stored = sems("p_stored", 2)
        rel_in = sems("rel_in", 2)
        pre_ready = sem("pre_ready")
        pre_added = sem("pre_added")
        pos_ready = sem("pos_ready")
        score_ready = sem("score_ready")
        masked = sem("masked")
        exp_ready = sem("exp_ready")
        exp_kept = sem("exp_kept")
        den_hot_ready = sem("den_hot_ready")
        den_added = sem("den_added")
        rden_ready = sem("rden_ready")
        rden_flipped = sem("rden_flipped")
        rden_kept = sem("rden_kept")
        x1_stored = sem("x1_stored")
        agg_zero = sem("agg_zero")
        sum_staged = sem("sum_staged")
        sum_flipped = sem("sum_flipped")
        y_ready = sem("y_ready")
        out_ready = sem("out_ready")
        out_stored = sems("out_stored", 2)
        passed = sem("passed")
        dve_own = sem("dve_own")

        CONSTS = 11
        CREDIT = GPI
        LAST = BLOCKS - 1
        PASS_A, PASS_B = LAYERS, LAYERS + 1

        def stand_alone(eng):
            eng.sem_inc(passed, 1)

        def block_pairs(eng, body):
            with eng.Fori(0, LAST // 2) as i:
                body([(2 * i, 0, i), (2 * i + 1, 1, i)], False)
            body([(LAST, 0, LAST // 2)], True)

        def x_rows(ap, b, tail):
            if not tail:
                return [(slice(0, P), slice(0, C), ap[ds(b * W, W), :].rearrange("(c p) d -> p c d", p=P))]
            n0 = LAST * W
            full = ap[n0:n0 + TAIL_C * P, :].rearrange("(c p) d -> p c d", p=P)
            part = ap[n0 + TAIL_C * P:N, :].rearrange("(c p) d -> p c d", c=1)
            return [(slice(0, P), slice(0, TAIL_C), full), (slice(0, TAIL_R), slice(TAIL_C, TAIL_C + 1), part)]

        X_TAIL = 2

        def x_loads(stage_no, s, uses, tail):
            per = (LAST // 2 + X_TAIL, LAST // 2)[s]
            return 16 * (stage_no * per + (per if tail else uses + 1))

        def stores(stage_no, s, uses):
            return 16 * (1 + stage_no * (LAST // 2 + (s == 0)) + uses)

        block = ctx.enter_context(nc.Block())

        @block.sync
        def _(sp):
            sp.sem_inc(table_out[0], 16)
            sp.sem_inc(table_out[1], 16)
            sp.sem_inc(p_stored[0], 16)
            sp.sem_inc(p_stored[1], 16)
            sp.sem_inc(out_stored[0], 16)
            sp.sem_inc(out_stored[1], 16)
            flat = "q e -> (q e)"
            for given, ours, pad in ((src, edge_src, pad_src), (dst, edge_dst, pad_dst)):
                sp.dma_start(ours.rearrange(flat)[0:E].rearrange("(p e) -> p e", p=EP),
                             given.rearrange("(p e) -> p e", p=EP)).then_inc(edges_in, 16)
            sp.dma_start(given_src, src.rearrange("(p e) -> p e", p=EP)).then_inc(given_in, 16)
            sp.dma_start(given_dst[:, 0:EC], dst.rearrange("(p e) -> p e", p=EP)).then_inc(given_in, 16)
            sp.wait_ge(consts, CONSTS)
            sp.dma_start(given_dst[0:EP - 1, EC:EC + 1], dst[EC:E].rearrange("(p e) -> p e", e=EC)[:, 0:1],
                         allow_slow_non_contiguous=True).then_inc(given_in, 16)
            for ours, pad in ((edge_src, pad_src), (edge_dst, pad_dst)):
                sp.dma_start(ours.rearrange(flat)[E:QPAD].rearrange("(p e) -> p e", p=PP),
                             pad).then_inc(edges_in, 16)
            sp.dma_start(eps1[:, 0:LAYERS], eps.rearrange("(o l) -> o l", o=1).to_broadcast([P, LAYERS])).then_inc(const_in, 16)
            sp.dma_start(a_row[:, :], a.rearrange("c o -> o c").to_broadcast([P, D])).then_inc(const_in, 16)
            sp.dma_start(w_s[:, :, :], w.rearrange("(h f) c -> f h c", h=2)).then_inc(const_in, 16)
            sp.wait_ge(edges_in, 64)
            sp.wait_ge(order_known, 1)
            with sp.If(sp.value_load(unordered[0:1, 0:1], min_val=0, max_val=E) > 0):
                sp.wait_ge(regrouped, 1)
            sp.dma_start(last_i[:, :], edge_dst[:, PAIR - 1:PAIR].rearrange("(r p) o -> p (r o)", p=P),
                         allow_slow_non_contiguous=True).then_inc(last_in, 16)

            def load_x(stage_no, b, s, tail):
                for p, c, rows_of_x in x_rows(x, b, tail):
                    sp.dma_start(x_in[p, s, c, :], rows_of_x).then_inc(x_loaded[s], 16)

            def store_table(stage_no, b, s):
                sp.wait_ge(split_done, 2 + stage_no * BLOCKS + b + 1)
                sp.dma_start(table_h[ds(b * W, W), :].rearrange("(c p) f -> p c f", p=P),
                             split[:, s, :, :]).then_inc(table_out[s], 16)

            def prepare(blocks, tail):
                for b, s, uses in blocks:
                    sp.wait_ge(split_done, b + 1)
                    sp.wait_ge(x_flipped, b + 1)
                    load_x(0, b, s, tail)
                for b, s, uses in blocks:
                    store_table(0, b, s)

            block_pairs(sp, prepare)

            sp.wait_ge(pairs_ready, 1)
            sp.dma_start(block_row.rearrange("o (r p) -> p (o r)", p=P), group_bi[:, :],
                         allow_slow_non_contiguous=True).then_inc(base_out, 16)
            sp.wait_ge(base_out, 16)
            sp.dma_start(base_row[:, :], block_row).then_inc(base_in, 16)
            sp.wait_ge(g_ready, 1)
            sp.dma_start(rel_rows.rearrange("(r p) e -> p r e", p=P), g_rel16).then_inc(rel_out, 16)

            def load_weights(l, ready):
                sp.wait_ge(h_flipped, ready)
                sp.dma_start(w1_s[:, :], w1[l, :, :]).then_inc(weights_in, 16)
                sp.dma_start(w2_s[:, :], w2[l, :, :]).then_inc(weights_in, 16)
                sp.dma_start(b1_s[:, :], b1[l, :].rearrange("(p o) -> p o", o=1)).then_inc(weights_in, 16)
                sp.dma_start(b2_s[:, :], b2[l, :].rearrange("(p o) -> p o", o=1)).then_inc(weights_in, 16)

            with sp.Fori(0, LAYERS - 1) as l:
                sp.wait_ge(h_flipped, 2 + l * BLOCKS)
                sp.dma_start(w1_s[:, :], w1[ds(l, 1), :, :].rearrange("o p f -> (o p) f")).then_inc(weights_in, 16)
                sp.dma_start(w2_s[:, :], w2[ds(l, 1), :, :].rearrange("o p f -> (o p) f")).then_inc(weights_in, 16)
                sp.dma_start(b1_s[:, :], b1[ds(l, 1), :].rearrange("o (p q) -> (o p) q", q=1)).then_inc(weights_in, 16)
                sp.dma_start(b2_s[:, :], b2[ds(l, 1), :].rearrange("o (p q) -> (o p) q", q=1)).then_inc(weights_in, 16)
                with sp.Fori(0, LAST // 2) as i:
                    for s in range(2):
                        store_table(l + 1, 2 * i + s, s)
                store_table(l + 1, LAST, 0)
            load_weights(LAYERS - 1, 2 + (LAYERS - 1) * BLOCKS)
            sp.wait_ge(bank_free, BANKS + LAYERS * G)

            def last_rows(blocks, tail):
                for b, s, uses in blocks:
                    sp.wait_ge(split_done, LAYERS * BLOCKS + b + 1)
                    load_x(1, b, s, tail)
                for b, s, uses in blocks:
                    sp.wait_ge(p_taken, 1 + b + 1)
                    sp.wait_ge(q_taken, 1 + b + 1)
                    sp.dma_start(table_p[ds(b * W, W), :].rearrange("(c p) f -> p c f", p=P),
                                 p_rows[:, s, :, :]).then_inc(p_stored[s], 16)

            block_pairs(sp, last_rows)

            sp.wait_ge(rel_out, 16)
            with sp.Fori(0, TURNS) as i:
                for h in range(2):
                    sp.wait_ge(hot_ready, LAYERS * G + i * GPI + (h - 1) * HALF)
                    sp.dma_start(rel_row[:, h, :], rel_rows[ds(i * GPI + h * HALF, HALF), :]
                                 .rearrange("(o g) e -> o (g e)", o=1).to_broadcast([P, HALF * PAIR])).then_inc(rel_in[h], 16)

            sp.wait_ge(rden_kept, 1)
            for k in range(2):
                c0, c1 = k * HI // 2, (k + 1) * HI // 2
                sp.dma_start(table_x1[c0 * P:c1 * P, :].rearrange("(c p) d -> p c d", p=P),
                             x1_rows[:, c0:c1, :]).then_inc(x1_stored, 16)

            def store_out(blocks, tail):
                for b, s, uses in blocks:
                    sp.wait_ge(out_ready, b + 1)
                    for p, c, rows_of_out in x_rows(out, b, tail):
                        sp.dma_start(rows_of_out, norm[p, s, c, :]).then_inc(out_stored[s], 16)

            block_pairs(sp, store_out)
            sp.wait_ge(out_stored[0], 16 * (1 + LAST // 2 + X_TAIL))
            sp.wait_ge(out_stored[1], 16 * (1 + LAST // 2))

        @block.gpsimd
        def _(pool):
            own = Count(pool, consts)
            own.add(pool.memset(ident[:, :], 0.0))
            own.add(pool.iota(iota_i, [[1, W]], base=0, channel_multiplier=0))
            own.add(pool.iota(node_i[:, :], [[P, C]], base=0, channel_multiplier=1))
            own.add(pool.iota(group_i[:, :], [[P, RG]], base=0, channel_multiplier=1))
            own.add(pool.iota(first_i[:, :], [[W, BLOCKS]], base=0, channel_multiplier=0))
            own.add(pool.memset(pad_src, 0))
            own.add(pool.memset(pad_dst, NPAD))
            own.add(pool.memset(p_rows[:, :, :, :], 0.0))
            own.add(pool.memset(given_dst[:, EC:EC + 1], NPAD))
            pool.wait_ge(consts, 1)
            pool.wait_ge(ones_set, 1)
            own.add(pool.affine_select(out=before, in_=ones[:, :], compare_op=ALU.is_gt, fill=0.0,
                                       base=0, pattern=[[1, P]], channel_multiplier=-1))
            own.add(pool.affine_select(out=ident[:, :], in_=ident[:, :], compare_op=ALU.not_equal, fill=1.0,
                                       base=0, pattern=[[-1, P]], channel_multiplier=1))
            assert own.k == CONSTS

            pool.wait_ge(edges_in, 64)
            pool.wait_ge(order_known, 1)
            with pool.If(pool.value_load(unordered[0:1, 0:1], min_val=0, max_val=E) > 0):
                with pool.Fori(0, EC) as t:
                    pool.wait_ge(edge_placed, t + 1)
                    stand_alone(pool)
                    for n, table in enumerate((edge_src, edge_dst)):
                        pool.indirect_dma_start(out=table.rearrange("q (e o) -> (q e) o", o=1),
                                                out_offset=bass.IndirectOffsetOnAxis(ap=edge_place_i[0:EP, 0:1], axis=0),
                                                in_=edge_now[0:EP, n:n + 1], in_offset=None).then_inc(edge_moved, 16)
                    pool.wait_ge(edge_moved, 32 * (t + 1))
                pool.sem_inc(regrouped, 1)

            pool.wait_ge(pairs_ready, 1)
            for r in range(RG):
                for table, to in ((edge_src, g_src), (edge_dst, g_dst)):
                    pool.indirect_dma_start(out=to[:, r, :], out_offset=None, in_=table,
                                            in_offset=bass.IndirectOffsetOnAxis(ap=pair_i[:, r:r + 1], axis=0)) \
                        .then_inc(edges_g, 16)

            def gather_pass(no, turn, table, to, freed, group0):
                for t in range(TPI):
                    if t % (TPI // 2) == 0:
                        pool.wait_ge(staged, 2 * (no * TURNS + turn) + t // (TPI // 2) + 1)
                    if t % 2 == 0:
                        pool.wait_ge(freed, group0 + turn * GPI + t // 2 + 1)
                        stand_alone(pool)
                    pool.indirect_dma_start(out=to(t), out_offset=None, in_=table,
                                            in_offset=bass.IndirectOffsetOnAxis(ap=idx_now[:, t:t + 1], axis=0)) \
                        .then_inc(row_in[t], 16)

            with pool.Fori(0, LAYERS) as l:
                for s in range(2):
                    pool.wait_ge(table_out[s], 16 * (1 + (l + 1) * (LAST // 2 + (s == 0))))
                stand_alone(pool)
                with pool.Fori(0, TURNS) as i:
                    gather_pass(l, i, table_h, lambda t: rows[:, t, :], group_summed, l * G)

            def keep(blocks, tail):
                for b, s, uses in blocks:
                    pool.wait_ge(norm_done, b + 1)
                    pool.tensor_copy(x1_rows[:, ds(b * C, C), 0:D], norm[:, s, :, :]).then_inc(x1_kept, 1)

            pool.wait_ge(g_taken, RG)
            pool.wait_ge(rel_out, 16)
            pool.memset(x1_rows[:, :, D:ROW1], 0.0).then_inc(x1_kept, 2)
            block_pairs(pool, keep)

            for s in range(2):
                pool.wait_ge(p_stored[s], 16 * (1 + LAST // 2 + (s == 0)))
            with pool.Fori(0, TURNS) as i:
                gather_pass(PASS_A, i, table_p, lambda t: rows_f[:, t, 0:ROW1], pre_added, 0)

            pool.wait_ge(pre_ready, BANKS + G)
            pool.memset(agg[:, NPAD // 2:NPAD], 0.0).then_inc(agg_zero, 1)
            pool.wait_ge(x1_stored, 32)
            with pool.Fori(0, TURNS) as i:
                gather_pass(PASS_B, i, table_x1, lambda t: rows_f[:, t, 0:ROW1], group_summed, LAYERS * G)

        @block.scalar
        def _(act):
            for free, n in ((x_taken, 2), (hid_done, 2), (h_done, 2), (x1_t_done, 2), (p_taken, 1),
                            (pos_ready, BANKS), (exp_ready, 1)):
                act.sem_inc(free, n)

            act.wait_ge(ones_set, 2)

            def first_sums(blocks, tail):
                for b, s, uses in blocks:
                    act.wait_ge(x_flipped, 2 + b + 1)
                    act.activation(agg[:, ds(b * W, W)], ps[4 + s][:, :], ACT.Copy,
                                   scale=eps1[:, 0:1]).then_inc(x_taken, 1)

            block_pairs(act, first_sums)

            def stage_turn(no, turn, freed, group0, what):
                for h in range(2):
                    act.wait_ge(freed, group0 + turn * GPI + (h + 1) * HALF)
                    c = slice(h * TPI // 2, (h + 1) * TPI // 2)
                    for of, to in what:
                        ins = act.activation(to[:, c], of[:, ds(turn * TPI + h * (TPI // 2), TPI // 2)], ACT.Copy)
                    ins.then_inc(staged, 1)

            act.wait_ge(g_taken, RG)

            def relu(nb, s):
                act.wait_ge(up_done, nb + 1)
                act.wait_ge(down_done, nb + 1)
                act.activation(hid[:, s, :], ps[6 + s][:, :], ACT.Relu, bias=b1_s[:, :]).then_inc(hid_done, 1)

            def take_h(nb, s, bank):
                act.wait_ge(down_done, 2 + nb + 1)
                act.wait_ge(h_flipped, nb + 1)
                act.activation(h_t[:, s, :], ps[bank][:, :], ACT.Identity, bias=b2_s[:, :]).then_inc(h_done, 1)

            with act.Fori(0, LAYERS - 1) as l:
                with act.Fori(0, TURNS) as i:
                    stage_turn(l, i, group_summed, l * G, ((src_t, idx_now), (rel_t, rel_now)))
                act.wait_ge(weights_in, 64 * (l + 1))

                def mlp(blocks, tail):
                    for b, s, uses in blocks:
                        relu(l * BLOCKS + b, s)
                    for b, s, uses in blocks:
                        nb = l * BLOCKS + b
                        take_h(nb, s, 4 + s)
                        act.wait_ge(h_done, 2 + nb + 1)
                        act.activation(agg[:, ds(b * W, W)], h_t[:, s, :], ACT.Copy,
                                       scale=eps1[:, ds(l + 1, 1)]).then_inc(agg_set, 1)

                block_pairs(act, mlp)
            with act.Fori(0, TURNS) as i:
                stage_turn(LAYERS - 1, i, group_summed, (LAYERS - 1) * G, ((src_t, idx_now), (rel_t, rel_now)))
            act.wait_ge(weights_in, 64 * LAYERS)

            def deviation(b, s):
                act.wait_ge(var_ready, b + 1)
                act.activation(std[:, s, :], mean_var[:, s, :, 1], ACT.Sqrt, bias=ln_eps[:, :]).then_inc(std_ready, 1)

            def mlp_norm(blocks, tail):
                n0 = (LAYERS - 1) * BLOCKS
                for b, s, uses in blocks:
                    relu(n0 + b, s)
                for b, s, uses in blocks:
                    take_h(n0 + b, s, 4)
                for b, s, uses in blocks:
                    deviation(b, s)
                for b, s, uses in blocks:
                    act.wait_ge(x1_flipped, 2 + b + 1)
                    act.wait_ge(pq_done, b + 1)
                    act.activation(x1_t[:, s, :], ps[6 + s][:, :], ACT.Copy).then_inc(x1_t_done, 1)
                for b, s, uses in blocks:
                    act.wait_ge(pq_done, 2 + b + 1)
                    act.wait_ge(p_stored[s], stores(0, s, uses))
                    act.activation(p_rows[:, s, :, 0:D], ps[0][:, :].rearrange("p (c d) -> p c d", c=C),
                                   ACT.Copy).then_inc(p_taken, 1)

            block_pairs(act, mlp_norm)

            with act.Fori(0, TURNS) as i:
                stage_turn(PASS_A, i, pre_added, 0, ((src_t, idx_now),))
                for j in range(GPI):
                    act.wait_ge(pre_added, CREDIT + i * GPI + j + 1)
                    act.wait_ge(score_ready, i * GPI + j + 1)
                    act.activation(pos[:, j % BANKS, :, :], pre[:, j % BANKS, :, 0:D], ACT.Relu).then_inc(pos_ready, 1)
                act.wait_ge(masked, i + 1)
                act.activation(exp_now[:, :], masked_s[:, :], ACT.Exp).then_inc(exp_ready, 1)
                act.wait_ge(exp_ready, 1 + i + 1)
                act.activation(exp_t[:, ds(i * TPI, TPI)], exp_now[:, :], ACT.Copy).then_inc(exp_kept, 1)

            act.wait_ge(exp_kept, TURNS)
            act.wait_ge(rden_ready, 1)
            with act.Fori(0, TURNS) as i:
                stage_turn(PASS_B, i, group_summed, LAYERS * G, ((src_t, idx_now), (rel_t, rel_now), (exp_t, exp_now)))

            act.wait_ge(bank_free, BANKS + (LAYERS + 1) * G)

            def take_sums(blocks, tail):
                for b, s, uses in blocks:
                    act.wait_ge(sum_flipped, b + 1)
                    act.activation(h_t[:, s, :], agg[:, ds(b * W, W)], ACT.Copy).then_inc(sum_staged, 1)
                for b, s, uses in blocks:
                    deviation(BLOCKS + b, s)

            block_pairs(act, take_sums)

        @block.tensor
        def _(pe):
            for free, n in ((group_summed, CREDIT), (pre_ready, BANKS), (x_flipped, 2), (down_done, 2), (h_flipped, 2),
                            (x1_flipped, 2), (pq_done, 2), (sum_flipped, 2), (den_added, 8)):
                pe.sem_inc(free, n)
            pe.wait_ge(ones_set, 1)
            pe.wait_ge(consts, CONSTS)
            pe.wait_ge(down_ready, 1)
            pe.matmul(ps[1][:, 0:1], ones[0:EP, :], steps_down[0:EP, :], start=True, stop=True).then_inc(down_summed, 1)
            pe.wait_ge(order_known, 1)
            with pe.If(pe.value_load(unordered[0:1, 0:1], min_val=0, max_val=E) > 0):
                pe.wait_ge(starts_ready, 1)
                pe.matmul(ps[0][0:EP, 0:BLOCKS], ones[0:EP, 0:EP], place[0:EP, :], start=True, stop=True).then_inc(starts_summed, 1)
                with pe.Fori(0, EC) as t:
                    pe.wait_ge(edge_hot_ready, t + 1)
                    pe.matmul(ps[1][0:EP, 0:BLOCKS], before[0:EP, 0:EP], edge_hot[0:EP, :], start=True, stop=True)
                    pe.matmul(ps[2][0:EP, 0:BLOCKS], ones[0:EP, 0:EP], edge_hot[0:EP, :], start=True, stop=True) \
                        .then_inc(edge_ranked, 1)

            pe.wait_ge(counted, 1)
            pe.matmul(ps[0][:, 0:RG * BLOCKS], ones[:, :], below[:, :, :].rearrange("p r b -> p (r b)"),
                      start=True, stop=True).then_inc(summed_b, 1)

            def flip(bank, rows_in):
                for c in range(C):
                    ins = pe.transpose(ps[bank][:, c * P:(c + 1) * P], rows_in(c), ident[:, :])
                return ins

            def flip_x(blocks, tail):
                for b, s, uses in blocks:
                    pe.wait_ge(x_loaded[s], x_loads(0, s, uses, tail))
                    pe.wait_ge(x_taken, b + 1)
                    flip(4 + s, lambda c: x_in[:, s, c, :]).then_inc(x_flipped, 1)

            block_pairs(pe, flip_x)

            pe.wait_ge(g_ready, 1)
            for r in range(RG):
                if r >= BANKS:
                    pe.wait_ge(g_taken, r - BANKS + 1)
                for n, of in enumerate((g_srcf, g_rel)):
                    for k in range(2):
                        m = 2 * n + k
                        ins = pe.transpose(ps[r % BANKS][:, m * P:(m + 1) * P], of[:, r, k * P:(k + 1) * P], ident[:, :])
                ins.then_inc(g_flipped, 1)
            pe.wait_ge(g_taken, RG)

            def sum_turn(turn_all, group0, turn, hot0, product):
                for j in range(GPI):
                    g = group0 + turn * GPI + j
                    pe.wait_ge(bank_free, g + 1)
                    pe.wait_ge(hot_ready, hot0 + turn * GPI + j + 1)
                    for k in range(2):
                        pe.wait_ge(row_in[2 * j + k], 16 * (turn_all + 1))
                        ins = product(j, k)
                    ins.then_inc(group_summed, 1)

            def product_h(j, k):
                for part in range(3):
                    ins = pe.matmul(ps[j % BANKS][:, :], rows[:, 2 * j + k, part * D:(part + 1) * D], hot_bf[:, j % BANKS, k, :],
                                    start=(k == 0 and part == 0), stop=(k == 1 and part == 2))
                return ins

            def product_x1(j, k):
                return pe.matmul(ps[j % BANKS][:, :], rows_f[:, 2 * j + k, 0:D], hot_w[:, j % BANKS, k, :],
                                 start=(k == 0), stop=(k == 1))

            def layer_sums(l):
                with pe.Fori(0, TURNS) as i:
                    sum_turn(l * TURNS + i, l * G, i, l * G, product_h)
                pe.wait_ge(bank_free, BANKS + (l + 1) * G)
                pe.wait_ge(weights_in, 64 * (l + 1))
                stand_alone(pe)

            def up(nb, b, s):
                pe.wait_ge(hid_done, nb + 1)
                pe.matmul(ps[6 + s][:, :], w1_s[:, :], agg[:, ds(b * W, W)], start=True, stop=True).then_inc(up_done, 1)

            def down(nb, s, bank, free):
                pe.wait_ge(hid_done, 2 + nb + 1)
                pe.wait_ge(h_done, nb + 1 + free)
                pe.matmul(ps[bank][:, :], w2_s[:, :], hid[:, s, :], start=True, stop=True).then_inc(down_done, 1)

            def flip_h(nb, s):
                pe.wait_ge(h_done, 2 + nb + 1)
                pe.wait_ge(split_done, BLOCKS + nb + 1)
                flip(2 + s, lambda c: h_t[:, s, c * P:(c + 1) * P]).then_inc(h_flipped, 1)

            with pe.Fori(0, LAYERS - 1) as l:
                layer_sums(l)

                def mlp(blocks, tail):
                    for b, s, uses in blocks:
                        up(l * BLOCKS + b, b, s)
                    for b, s, uses in blocks:
                        down(l * BLOCKS + b, s, 4 + s, 0)
                    for b, s, uses in blocks:
                        flip_h(l * BLOCKS + b, s)

                block_pairs(pe, mlp)
                pe.wait_ge(split_done, 2 + (l + 2) * BLOCKS)
                stand_alone(pe)
            layer_sums(LAYERS - 1)

            def mlp_norm(blocks, tail):
                n0 = (LAYERS - 1) * BLOCKS
                for b, s, uses in blocks:
                    pe.wait_ge(x1_t_done, b + 1)
                    up(n0 + b, b, s)
                for b, s, uses in blocks:
                    down(n0 + b, s, 4, 1)
                for b, s, uses in blocks:
                    flip_h(n0 + b, s)
                for b, s, uses in blocks:
                    pe.wait_ge(norm_done, b + 1)
                    flip(6 + s, lambda c: norm[:, s, c, :]).then_inc(x1_flipped, 1)
                for b, s, uses in blocks:
                    pe.wait_ge(x1_t_done, 2 + b + 1)
                    pe.wait_ge(p_taken, b + 1)
                    pe.wait_ge(q_taken, b + 1)
                    for c in range(C):
                        chunk = x1_t[:, s, c * P:(c + 1) * P]
                        pe.matmul(ps[0][:, c * D:(c + 1) * D], chunk, w_s[:, 0, :], start=True, stop=True)
                        pe.matmul(ps[1][:, c * D:(c + 1) * D], chunk, w_s[:, 1, :], start=True, stop=True)
                        ins = pe.matmul(ps[5][:, 2 * c:2 * c + 2], chunk, wa_s[:, :], start=True, stop=True)
                    ins.then_inc(pq_done, 1)

            block_pairs(pe, mlp_norm)
            pe.wait_ge(p_taken, 1 + BLOCKS)
            pe.wait_ge(q_taken, 1 + BLOCKS)

            def add_den(t, n, last=False):
                pe.wait_ge(den_hot_ready, n + 1)
                pe.matmul(den_ps[0:HI, :], den_hot[:, t % 8, 0, 0:HI], den_hot[:, t % 8, 1, :],
                          start=False, stop=False).then_inc(den_added, 1)

            pe.matmul(den_ps[0:HI, :], zeros[:, 0:HI], zeros[:, :], start=True, stop=False)
            with pe.Fori(0, TURNS) as i:
                _, blocks_now = nc.values_load_multi_w_load_instructions(
                    base_row[0:1, ds(i * GPI, GPI)], engines=(mybir.EngineType.PE,), min_val=0, max_val=LAST,
                    skip_runtime_bounds_check_because="a group's block, by its making")
                for j in range(GPI):
                    g = i * GPI + j
                    pe.wait_ge(pre_added, g + BANKS + 1)
                    pe.wait_ge(hot_ready, LAYERS * G + g + 1)
                    q0 = blocks_now[j] * (C * ROW1)
                    for k in range(2):
                        for c in range(C):
                            ins = pe.matmul(ps[j % BANKS][:, k * (D + 1):(k + 1) * (D + 1)],
                                            hot_t[:, j % BANKS, c, k * P:(k + 1) * P],
                                            big[:, ds(q0 + c * ROW1, D + 1)], start=(c == 0), stop=(c == C - 1))
                    ins.then_inc(pre_ready, 1)
                    for t in (2 * j, 2 * j + 1):
                        add_den(t, i * TPI + t)
            for t in range(TPI):
                add_den(t, TURNS * TPI + t)
            pe.matmul(den_ps[0:HI, :], zeros[:, 0:HI], zeros[:, :], start=False, stop=True).then_inc(den_added, 1)
            pe.wait_ge(rden_ready, 1)
            pe.transpose(ps[5][:, 0:HI], den_s[0:HI, 1, :], ident[0:HI, 0:HI]).then_inc(rden_flipped, 1)

            with pe.Fori(0, TURNS) as i:
                sum_turn(PASS_B * TURNS + i, LAYERS * G, i, (LAYERS + 1) * G, product_x1)
            pe.wait_ge(bank_free, BANKS + (LAYERS + 1) * G)

            def flip_sums(blocks, tail):
                for b, s, uses in blocks:
                    pe.wait_ge(sum_staged, b + 1)
                    pe.wait_ge(y_ready, b + 1)
                    flip(2 + s, lambda c: h_t[:, s, c * P:(c + 1) * P]).then_inc(sum_flipped, 1)

            block_pairs(pe, flip_sums)

        @block.vector
        def _(dve):
            own = Count(dve, dve_own)
            for free, n in ((bank_free, BANKS), (pre_added, CREDIT), (split_done, 2), (q_taken, 1), (score_ready, BANKS),
                            (y_ready, 2)):
                dve.sem_inc(free, n)
            dve.memset(zeros[:, :], 0.0)
            dve.memset(exp_now[:, :], 0.0)
            dve.memset(hilo[:, :, :], 0.0)
            dve.memset(ln_eps[:, :], LN_EPS)
            dve.memset(ones[:, :], 1.0).then_inc(ones_set, 1)
            dve.wait_ge(consts, CONSTS)
            dve.tensor_copy(iota_f[:, :], iota_i)
            dve.tensor_copy(iota16[:, :], iota_i)
            dve.tensor_copy(node_c[:, :], node_i[:, :])
            dve.tensor_copy(group_c[:, :], group_i[:, :])
            own.add(dve.tensor_copy(first_f[:, :], first_i[:, :]))
            own.wait()
            own.add(dve.tensor_scalar(block_f[:, :], first_f[:, :], 1.0 / W, None, ALU.mult))
            dve.wait_ge(given_in, 48)
            own.add(dve.tensor_single_scalar(given_bi, given_dst, W.bit_length() - 1, ALU.logical_shift_right))
            own.wait()
            own.add(dve.tensor_copy(given_b, given_bi))
            own.wait()
            own.add(dve.tensor_tensor(given_down, given_b[:, 1:EC + 1], given_b[:, 0:EC], ALU.is_lt))
            own.wait()
            dve.reduce_sum(steps_down[0:EP, :], given_down, axis=AX).then_inc(down_ready, 1)
            dve.wait_ge(down_summed, 1)
            dve.tensor_copy(unordered[:, :], ps[1][0:1, 0:1]).then_inc(order_known, 1)
            dve.wait_ge(order_known, 1)
            with dve.If(dve.value_load(unordered[0:1, 0:1], min_val=0, max_val=E) > 0):
                outside_own = (own.base, own.k)
                for b in range(BLOCKS):
                    own.add(dve.tensor_scalar(given_down, given_b[:, 0:EC], float(b), 0.0, ALU.is_lt, ALU.add,
                                              accum_out=place[0:EP, b:b + 1]))
                    own.wait()
                dve.sem_inc(starts_ready, 1)
                dve.wait_ge(starts_summed, 1)
                own.add(dve.tensor_copy(place[0:EP, :], ps[0][0:EP, 0:BLOCKS]))
                own.wait()
                with dve.Fori(0, EC) as t:
                    own.enter(t, 6)
                    own.wait()
                    dve.tensor_scalar(edge_hot[0:EP, :], block_f[0:EP, :], given_b[:, ds(t, 1)], None, ALU.is_equal) \
                        .then_inc(edge_hot_ready, 1)
                    own.add(dve.tensor_copy(edge_now[0:EP, 0:1], given_src[:, ds(t, 1)]))
                    own.add(dve.tensor_copy(edge_now[0:EP, 1:2], given_dst[:, ds(t, 1)]))
                    dve.wait_ge(edge_ranked, t + 1)
                    own.add(dve.tensor_tensor(edge_rank[0:EP, :], ps[1][0:EP, 0:BLOCKS], place[0:EP, :], ALU.add))
                    own.wait()
                    own.add(dve.tensor_tensor(place[0:EP, :], ps[2][0:EP, 0:BLOCKS], place[0:EP, :], ALU.add))
                    own.add(dve.tensor_tensor(edge_rank[0:EP, :], edge_rank[0:EP, :], edge_hot[0:EP, :], ALU.mult))
                    own.wait()
                    own.add(dve.reduce_sum(edge_place[0:EP, :], edge_rank[0:EP, :], axis=AX))
                    own.wait()
                    dve.tensor_copy(edge_place_i[0:EP, :], edge_place[0:EP, :]).then_inc(edge_placed, 1)
                    dve.wait_ge(edge_moved, 32 * (t + 1))
                    own.leave(EC)
                regroup_adds = own.base + own.k - sum(outside_own)
            with dve.Else():
                dve.sem_inc(dve_own, regroup_adds)
            dve.wait_ge(const_in, 48)
            for h in range(2):
                own.add(dve.tensor_tensor_reduce(out=junk, in0=w_s[:, h, :], in1=a_row[:, :], scale=NEG_SLOPE, scalar=0.0,
                                                 op0=ALU.mult, op1=ALU.add, accum_out=wa_s[:, h:h + 1]))
                own.wait()
            dve.tensor_scalar(a_08[:, :], a_row[:, :], 1.0 - NEG_SLOPE, None, ALU.mult)
            dve.tensor_scalar(eps1[:, :], eps1[:, :], 1.0, None, ALU.add).then_inc(ones_set, 1)

            dve.wait_ge(last_in, 16)
            own.add(dve.tensor_copy(last_f[:, :], last_i[:, :]))
            own.wait()
            for r in range(RG):
                ins = dve.tensor_scalar(below[:, r, :], first_f[:, :], last_f[:, r:r + 1], None, ALU.is_gt)
            ins.then_inc(counted, 1)
            dve.wait_ge(summed_b, 1)
            own.add(dve.tensor_reduce(start[:, :], ps[0][:, 0:RG * BLOCKS].rearrange("p (r b) -> p b r", r=RG), axis=AX, op=ALU.add))
            own.wait()
            own.add(dve.tensor_tensor(start[:, :], start[:, :], block_f[:, :], ALU.add))
            own.wait()
            for r in range(RG):
                own.add(dve.tensor_scalar(junk[:, 0:LAST], start[:, 1:BLOCKS], group_c[:, r:r + 1], 0.0, ALU.is_le, ALU.add,
                                          accum_out=group_b[:, r:r + 1]))
                own.wait()
            dve.tensor_copy(group_bi[:, :], group_b[:, :])
            dve.tensor_scalar(group_b512[:, :], group_b[:, :], float(W), None, ALU.mult)
            own.add(dve.tensor_tensor(pair_f[:, :], group_c[:, :], group_b[:, :], ALU.subtract))
            own.wait()
            dve.tensor_copy(pair_i[:, :], pair_f[:, :]).then_inc(pairs_ready, 1)

            def split_rows(u, of, s, uses):
                dve.wait_ge(table_out[s], stores(u, s, uses))
                own.add(dve.tensor_copy(split[:, s, :, 0:D], of))
                own.wait()
                own.add(dve.tensor_tensor(rest, of, split[:, s, :, 0:D], ALU.subtract))
                own.wait()
                own.add(dve.tensor_copy(split[:, s, :, D:2 * D], rest))
                own.wait()
                dve.tensor_tensor(split[:, s, :, 2 * D:3 * D], rest, split[:, s, :, D:2 * D],
                                  ALU.subtract).then_inc(split_done, 1)

            with dve.Fori(0, LAST // 2) as i:
                own.enter(i, 6)
                for s in range(2):
                    dve.wait_ge(x_loaded[s], x_loads(0, s, i, False))
                    split_rows(0, x_in[:, s, :, :], s, i)
                own.leave(LAST // 2)
            dve.wait_ge(x_loaded[0], x_loads(0, 0, LAST // 2, True))
            split_rows(0, x_in[:, 0, :, :], 0, LAST // 2)

            dve.wait_ge(edges_g, 16 * 2 * RG)
            dve.tensor_copy(g_srcf, g_src)
            for r in range(RG):
                ins = dve.tensor_scalar(g_rel[:, r, :], g_dst[:, r, :], group_b512[:, r:r + 1], None, ALU.subtract)
            own.add(ins)
            own.wait()
            dve.tensor_copy(g_rel16, g_rel).then_inc(g_ready, 1)
            for r in range(RG):
                n = min(P, G - r * P)
                dve.wait_ge(g_flipped, r + 1)
                for m, to in ((0, src_t), (1, rel_t)):
                    ins = dve.tensor_copy(to[:, 2 * r * P:2 * (r * P + n)].rearrange("p (g k) -> p k g", k=2),
                                          ps[r % BANKS][:, m * PAIR:(m + 1) * PAIR].rearrange("p (k g) -> p k g", k=2)[:, :, 0:n])
                ins.then_inc(g_taken, 1)
            dve.wait_ge(base_in, 16)

            def load_blocks(turn):
                _, values = nc.values_load_multi_w_load_instructions(
                    base_row[0:1, ds(turn * GPI, GPI)], engines=(mybir.EngineType.DVE,), min_val=0, max_val=LAST,
                    skip_runtime_bounds_check_because="a group's block, by its making")
                return values

            def add_group(g, j, b):
                dve.wait_ge(group_summed, CREDIT + g + 1)
                dve.wait_ge(bank_free, BANKS + g)
                sums = agg[:, ds(b * W, W)]
                dve.tensor_tensor(sums, sums, ps[j % BANKS][:, :], ALU.add).then_inc(bank_free, 1)

            def sum_turn(pass_no, group0, turn, one_hot):
                b = load_blocks(turn)
                for j in range(GPI):
                    if j % HALF == 0:
                        dve.wait_ge(staged, 2 * (pass_no * TURNS + turn) + j // HALF + 1)
                    dve.wait_ge(group_summed, group0 + turn * GPI + j + 1 + CREDIT - BANKS)
                    one_hot(j)
                    if j >= 2:
                        add_group(group0 + turn * GPI + j - 2, j - 2, b[j - 2])
                for j in (GPI - 2, GPI - 1):
                    add_group(group0 + turn * GPI + j, j, b[j])

            def hot_h(j):
                for k in range(2):
                    ins = dve.tensor_scalar(hot_bf[:, j % BANKS, k, :], iota16[:, :], rel_now[:, 2 * j + k:2 * j + k + 1],
                                            None, ALU.is_equal)
                ins.then_inc(hot_ready, 1)

            def layer_sums(l):
                dve.wait_ge(x_taken, 2 + BLOCKS)
                dve.wait_ge(split_done, 2 + (l + 1) * BLOCKS)
                stand_alone(dve)
                with dve.Fori(0, TURNS) as i:
                    sum_turn(l, l * G, i, hot_h)

            with dve.Fori(0, LAYERS - 1) as l:
                layer_sums(l)
                own.enter(l, 3 * BLOCKS)
                with dve.Fori(0, LAST // 2) as i:
                    own.enter(i, 6)
                    for s in range(2):
                        dve.wait_ge(h_flipped, 2 + l * BLOCKS + 2 * i + s + 1)
                        split_rows(l + 1, ps[2 + s][:, :].rearrange("p (c d) -> p c d", c=C), s, i)
                    own.leave(LAST // 2)
                dve.wait_ge(h_flipped, 2 + l * BLOCKS + BLOCKS)
                split_rows(l + 1, ps[2][:, :].rearrange("p (c d) -> p c d", c=C), 0, LAST // 2)
                dve.wait_ge(agg_set, (l + 1) * BLOCKS)
                own.leave(LAYERS - 1)
            layer_sums(LAYERS - 1)

            def moments(s, done, value):
                dve.wait_ge(done, value)
                for c in range(C):
                    ins = dve.bn_stats(stats[:, c, :], y[:, s, c, :])
                own.add(ins)
                own.wait()
                stand_alone(dve)
                for c in range(C):
                    ins = dve.bn_aggr(mean_var[:, s, c, :], stats[:, c, :])
                ins.then_inc(var_ready, 1)

            def normalise(b, s):
                dve.wait_ge(var_ready, b + 1)
                dve.wait_ge(std_ready, b + 1)
                own.add(dve.reciprocal(rstd[:, s, :], std[:, s, :]))
                own.wait()
                for c in range(C):
                    ins = dve.tensor_scalar(norm[:, s, c, :], y[:, s, c, :], mean_var[:, s, c, 0:1], rstd[:, s, c:c + 1],
                                            ALU.subtract, ALU.mult)
                return ins

            def x1_blocks(blocks, tail):
                n0 = (LAYERS - 1) * BLOCKS
                for b, s, uses in blocks:
                    dve.wait_ge(x_loaded[s], x_loads(1, s, uses, tail))
                    dve.wait_ge(h_flipped, 2 + n0 + b + 1)
                    dve.tensor_tensor(y[:, s, :, :], ps[2 + s][:, :].rearrange("p (c d) -> p c d", c=C), x_in[:, s, :, :],
                                      ALU.add).then_inc(split_done, 1)
                    moments(s, split_done, 2 + LAYERS * BLOCKS + b + 1)
                for b, s, uses in blocks:
                    dve.wait_ge(x1_flipped, b + 1)
                    dve.wait_ge(x1_kept, b + 1)
                    normalise(b, s).then_inc(norm_done, 1)
                for b, s, uses in blocks:
                    dve.wait_ge(pq_done, 2 + b + 1)
                    dve.wait_ge(p_stored[s], stores(0, s, uses))
                    q = big[:, ds(b * (C * ROW1), C * ROW1)].rearrange("p (c d) -> p c d", c=C)
                    dve.tensor_copy(q[:, :, 0:D], ps[1][:, :].rearrange("p (c d) -> p c d", c=C))
                    linear = ps[5][:, 0:2 * C].rearrange("p (c h) -> p c h", h=2)
                    dve.tensor_copy(q[:, :, D:D + 1], linear[:, :, 1:2])
                    dve.tensor_copy(p_rows[:, s, :, D:D + 1], linear[:, :, 0:1]).then_inc(q_taken, 1)

            with dve.Fori(0, LAST // 2) as i:
                own.enter(i, 4)
                x1_blocks([(2 * i, 0, i), (2 * i + 1, 1, i)], False)
                own.leave(LAST // 2)
            x1_blocks([(LAST, 0, LAST // 2)], True)

            def den_tile(t, n):
                dve.wait_ge(den_added, n + 1)
                dve.tensor_scalar(den_hot[:, t % 8, 0, 0:HI], iota_f[:, 0:HI], hilo[:, 0, t:t + 1], exp_now[:, t:t + 1],
                                  ALU.is_equal, ALU.mult)
                dve.tensor_scalar(den_hot[:, t % 8, 1, :], iota_f[:, 0:P], hilo[:, 1, t:t + 1], None,
                                  ALU.is_equal).then_inc(den_hot_ready, 1)

            def add_rows(i, j):
                g = i * GPI + j
                dve.wait_ge(pre_ready, BANKS + g + 1)
                for k in range(2):
                    dve.wait_ge(row_in[2 * j + k], 16 * (PASS_A * TURNS + i + 1))
                dve.wait_ge(pos_ready, g + 1)
                dve.tensor_tensor(pre[:, j % BANKS, :, 0:D + 1], ps[j % BANKS][:, 0:2 * (D + 1)].rearrange("p (k d) -> p k d", k=2),
                                  rows_f[:, 2 * j:2 * j + 2, 0:D + 1], ALU.add).then_inc(pre_added, 1)

            def scores(i, j):
                dve.wait_ge(pos_ready, BANKS + i * GPI + j + 1)
                for k in range(2):
                    ins = dve.tensor_tensor_reduce(out=pos[:, j % BANKS, k, :], in0=pos[:, j % BANKS, k, :], in1=a_08[:, :], scale=1.0,
                                                   scalar=pre[:, j % BANKS, k, D:D + 1], op0=ALU.mult, op1=ALU.add,
                                                   accum_out=score[:, 2 * j + k:2 * j + k + 1])
                ins.then_inc(score_ready, 1)

            dve.wait_ge(x1_kept, 2 + BLOCKS)
            with dve.Fori(0, TURNS) as i:
                own.enter(i, 6)
                dve.wait_ge(exp_ready, i + 1)
                for j in range(GPI):
                    g = i * GPI + j
                    if j % HALF == 0:
                        dve.wait_ge(rel_in[j // HALF], 16 * (i + 1))
                    dve.wait_ge(pre_ready, g + 1)
                    for c in range(C):
                        ins = dve.tensor_scalar(hot_t[:, j % BANKS, c, :], rel_row[:, j // HALF, (j % HALF) * PAIR:(j % HALF + 1) * PAIR],
                                                node_c[:, c:c + 1], None, ALU.is_equal)
                    ins.then_inc(hot_ready, 1)
                    den_tile(2 * j, i * TPI + 2 * j)
                    den_tile(2 * j + 1, i * TPI + 2 * j + 1)
                    if j >= 1:
                        add_rows(i, j - 1)
                    if j >= 2:
                        scores(i, j - 2)
                add_rows(i, GPI - 1)
                scores(i, GPI - 2)
                scores(i, GPI - 1)
                dve.tensor_single_scalar(hilo_i[:, 0, :], src_t[:, ds(i * TPI, TPI)], 7, ALU.logical_shift_right)
                own.add(dve.tensor_single_scalar(hilo_i[:, 1, :], src_t[:, ds(i * TPI, TPI)], P - 1, ALU.bitwise_and))
                own.add(dve.tensor_copy(rel_turn[:, :], rel_t[:, ds(i * TPI, TPI)]))
                own.wait()
                dve.tensor_copy(hilo[:, :, :], hilo_i[:, :, :])
                own.add(dve.tensor_scalar(inside[:, :], rel_turn[:, :], 0.0, None, ALU.is_ge))
                own.wait()
                own.add(dve.scalar_tensor_tensor(inside[:, :], rel_turn[:, :], float(W), inside[:, :], ALU.is_lt, ALU.mult))
                own.wait()
                dve.wait_ge(score_ready, BANKS + (i + 1) * GPI)
                own.add(dve.tensor_scalar(outside[:, :], inside[:, :], 1e30, -1e30, ALU.mult, ALU.add))
                own.add(dve.tensor_tensor(score[:, :], score[:, :], inside[:, :], ALU.mult))
                own.wait()
                dve.tensor_tensor(masked_s[:, :], score[:, :], outside[:, :], ALU.add).then_inc(masked, 1)
                own.leave(TURNS)
            dve.wait_ge(exp_ready, TURNS + 1)
            for t in range(TPI):
                den_tile(t, TURNS * TPI + t)
            dve.wait_ge(den_added, 8 + (TURNS + 1) * TPI + 1)
            own.add(dve.tensor_scalar(den_s[0:HI, 0, :], den_ps[0:HI, :], float(np.finfo(np.float32).tiny), None, ALU.max))
            own.wait()
            dve.reciprocal(den_s[0:HI, 1, :], den_s[0:HI, 0, :]).then_inc(rden_ready, 1)
            dve.wait_ge(rden_flipped, 1)
            dve.wait_ge(x1_kept, 2 + BLOCKS)
            dve.tensor_copy(x1_rows[:, 0:HI, D], ps[5][:, 0:HI]).then_inc(rden_kept, 1)
            dve.wait_ge(pre_ready, BANKS + G)
            own.add(dve.memset(agg[:, 0:NPAD // 2], 0.0))
            own.wait()
            dve.wait_ge(agg_zero, 1)

            with dve.Fori(0, TURNS) as i:
                own.enter(i, GPI)

                def hot_x1(j):
                    for k in range(2):
                        dve.wait_ge(row_in[2 * j + k], 16 * (PASS_B * TURNS + i + 1))
                    own.add(dve.tensor_tensor(att[:, 2 * j:2 * j + 2], rows_f[:, 2 * j:2 * j + 2, D], exp_now[:, 2 * j:2 * j + 2], ALU.mult))
                    own.wait()
                    for k in range(2):
                        t = 2 * j + k
                        ins = dve.tensor_scalar(hot_w[:, j % BANKS, k, :], iota_f[:, :], rel_now[:, t:t + 1], att[:, t:t + 1],
                                                ALU.is_equal, ALU.mult)
                    ins.then_inc(hot_ready, 1)

                sum_turn(PASS_B, LAYERS * G, i, hot_x1)
                own.leave(TURNS)

            def out_blocks(blocks, tail):
                for b, s, uses in blocks:
                    dve.wait_ge(sum_flipped, 2 + b + 1)
                    dve.tensor_tensor(y[:, s, :, :], ps[2 + s][:, :].rearrange("p (c d) -> p c d", c=C),
                                      x1_rows[:, ds(b * C, C), 0:D], ALU.add).then_inc(y_ready, 1)
                    moments(s, y_ready, 2 + b + 1)
                for b, s, uses in blocks:
                    dve.wait_ge(out_stored[s], stores(0, s, uses))
                    normalise(BLOCKS + b, s).then_inc(out_ready, 1)

            with dve.Fori(0, LAST // 2) as i:
                own.enter(i, 4)
                out_blocks([(2 * i, 0, i), (2 * i + 1, 1, i)], False)
                own.leave(LAST // 2)
            out_blocks([(LAST, 0, LAST // 2)], True)


_INS = ["x", "src", "dst", "L0_gnn_W1", "L0_gnn_b1", "L0_gnn_W2", "L0_gnn_b2", "L0_gnn_eps", "L1_gnn_w", "L1_gnn_a"]


def kernel(**inputs):
    import concourse.bacc as bacc
    from concourse.bass_utils import run_bass_kernel_spmd

    nc = bacc.Bacc("TRN2", target_bir_lowering=False, num_devices=1)
    arrays, args = {}, []
    for name in _INS:
        given = np.ascontiguousarray(inputs[name])
        arrays[f"in_{name}"] = given
        args.append(nc.dram_tensor(f"in_{name}", given.shape, mybir.dt.from_np(given.dtype), kind="ExternalInput").ap())
    out = nc.dram_tensor("out", (N, D), f32, kind="ExternalOutput").ap()
    gnn(nc, *args, out)
    return run_bass_kernel_spmd(nc, [arrays], core_ids=[0]).results[0]["out"]
```

```python
from contextlib import ExitStack

import numpy as np

import concourse.bass as bass
from concourse import mybir
from concourse.alu_op_type import AluOpType as ALU

f32 = mybir.dt.float32
bf16 = mybir.dt.bfloat16
i32 = mybir.dt.int32
i16 = mybir.dt.int16
ACT = mybir.ActivationFunctionType
AX = mybir.AxisListType.X

P = 128
D = 128
N = 12500
E = 200000
LAYERS = 3
W = 512
C = W // P
BLOCKS = -(-N // W)
TAIL = N - (BLOCKS - 1) * W
TAIL_C = TAIL // P
TAIL_R = TAIL - TAIL_C * P
NPAD = BLOCKS * W
PAIR = 2 * P
GPI = 8
TPI = 2 * GPI
HALF = GPI // 2
TURNS = -(-(E // PAIR + BLOCKS) // GPI)
G = TURNS * GPI
RG = -(-G // P)
QPAD = RG * P * PAIR
BANKS = 4
ROW1 = D + 1
SPLIT = 3 * D
PW = D + 1
Q_PART = D + 2
Q_SPLIT = 3 * Q_PART
P_SPLIT = 3 * PW
SLOT = P_SPLIT + 1
AGG0 = NPAD // P * Q_SPLIT // 2 - NPAD
NEG_SLOPE = 0.2
LN_EPS = 1e-5
EP = 125
EC = E // EP
assert EP * EC == E and RG * P >= G


class Count:

    def __init__(self, eng, sem):
        self.eng, self.sem, self.base, self.k, self.outer = eng, sem, 0, 0, []

    def add(self, ins):
        ins.then_inc(self.sem, 1)
        self.k += 1

    def wait(self):
        self.eng.wait_ge(self.sem, self.base + self.k)

    def enter(self, turn, per_turn):
        self.outer.append((self.base, self.k, per_turn))
        self.base, self.k = self.base + self.k + turn * per_turn, 0

    def leave(self, turns):
        base, k, per_turn = self.outer.pop()
        assert self.k == per_turn, f"a turn adds {self.k}, not {per_turn}"
        self.base, self.k = base, k + turns * per_turn


def gnn(nc, x, src, dst, w1, b1, w2, b2, eps, w, a, out):
    ctx = ExitStack()
    with ctx:
        def sb(name, shape, dt):
            return ctx.enter_context(nc.sbuf_tensor(name, shape, dt))

        def sem(name):
            return ctx.enter_context(nc.semaphore(name))

        def sems(name, n):
            return [sem(f"{name}{i}") for i in range(n)]

        ds = bass.ds

        edge_src = nc.dram_tensor("edge_src", (QPAD // PAIR, PAIR), i32).ap()
        edge_dst = nc.dram_tensor("edge_dst", (QPAD // PAIR, PAIR), i32).ap()
        block_row = nc.dram_tensor("block_row", (1, RG * P), i32).ap()
        rel_rows = nc.dram_tensor("rel_rows", (RG * P, PAIR), i16).ap()
        table_h = nc.dram_tensor("table_h", (NPAD, SPLIT), bf16).ap()
        table_p = nc.dram_tensor("table_p", (NPAD, P_SPLIT), bf16).ap()
        table_x1 = nc.dram_tensor("table_x1", (-(-N // P) * P, ROW1), f32).ap()

        big = sb("big", [P, AGG0 + NPAD], f32)
        q_rows = big[:, :].bitcast(bf16)
        agg = big[:, AGG0:AGG0 + NPAD]
        x1_rows = sb("x1_rows", [P, BLOCKS * C, ROW1], f32)
        room = x1_rows[:, :, :].rearrange("p c d -> p (c d)")
        QW = RG * PAIR
        g_src = room[:, 0:QW].bitcast(i32).rearrange("p (r e) -> p r e", r=RG)
        g_dst = room[:, QW:2 * QW].bitcast(i32).rearrange("p (r e) -> p r e", r=RG)
        g_srcf = room[:, 2 * QW:3 * QW].rearrange("p (r e) -> p r e", r=RG)
        g_rel = room[:, 3 * QW:4 * QW].rearrange("p (r e) -> p r e", r=RG)
        g_rel16 = room[:, 4 * QW:4 * QW + QW // 2].bitcast(i16).rearrange("p (r e) -> p r e", r=RG)
        given_src = room[0:EP, 0:EC].bitcast(i32)
        given_dst = room[0:EP, EC:2 * EC + 1].bitcast(i32)
        given_bi = room[0:EP, 2 * EC + 1:3 * EC + 2].bitcast(i32)
        given_b = room[0:EP, 3 * EC + 2:4 * EC + 3]
        given_down = room[0:EP, 4 * EC + 3:5 * EC + 3]
        assert 5 * EC + 3 <= 5 * QW
        PP, PC = 96, 306
        pad_src = room[0:PP, 5 * QW:5 * QW + PC].bitcast(i32)
        pad_dst = room[0:PP, 5 * QW + PC:5 * QW + 2 * PC].bitcast(i32)
        iota_i = room[:, 5 * QW + 2 * PC:5 * QW + 2 * PC + W].bitcast(i32)
        assert PP * PC == QPAD - E and 5 * QW + 2 * PC + W <= BLOCKS * C * ROW1
        src_t = sb("src_t", [P, 2 * G], i32)
        rel_t = sb("rel_t", [P, 2 * G], f32)
        exp_t = sb("exp_t", [P, TPI + 2 * G], f32)

        rows = sb("rows", [P, TPI, SLOT], bf16)
        rows_f = rows[:, :, :].bitcast(f32)
        hot = sb("hot", [P, BANKS, 2 * W], f32)
        hot_bf = hot[:, :, 0:W].bitcast(bf16).rearrange("p s (k w) -> p s k w", k=2)
        hot_w = hot[:, :, :].rearrange("p s (k w) -> p s k w", k=2)
        hot_t = hot[:, :, :].bitcast(bf16).rearrange("p s (c e) -> p s c e", c=C)
        between = hot[:, :, :].rearrange("p s w -> p (s w)")
        x_in = between[:, 0:2 * W].rearrange("p (s c d) -> p s c d", s=2, c=C)
        y = between[:, 2 * W:4 * W].rearrange("p (s c d) -> p s c d", s=2, c=C)
        rest = between[:, 4 * W:4 * W + C * Q_PART].rearrange("p (c d) -> p c d", c=C)
        p_f = between[:, 5 * W + P:5 * W + P + 2 * C * PW].rearrange("p (s c d) -> p s c d", s=2, c=C)
        den_s = between[:, 5 * W + P:5 * W + 2 * P]
        idx_now = sb("idx_now", [P, TPI], i32)
        rel_now = sb("rel_now", [P, TPI], f32)
        exp_now = sb("exp_now", [P, TPI], f32)

        stage = sb("stage", [P, 8 * W + P], f32)
        hid = stage[:, 0:2 * W].rearrange("p (s w) -> p s w", s=2)
        h_t = stage[:, 2 * W:4 * W].rearrange("p (s w) -> p s w", s=2)
        norm = stage[:, 4 * W:6 * W].rearrange("p (s c d) -> p s c d", s=2, c=C)
        x1_t = stage[:, 6 * W:8 * W].rearrange("p (s w) -> p s w", s=2)
        DEN = 8 * 2 * P
        den_hot = stage[:, 0:DEN].rearrange("p (s h n) -> p s h n", s=8, h=2)
        pos = stage[:, DEN:DEN + BANKS * PAIR].rearrange("p (s k d) -> p s k d", s=BANKS, k=2)
        assert DEN + BANKS * PAIR <= 8 * W + P

        split = sb("split", [P, 2, C * P_SPLIT], bf16)
        h_parts = split[:, :, 0:C * SPLIT].rearrange("p s (c f) -> p s c f", c=C)
        p_parts = split[:, :, :].rearrange("p s (c f) -> p s c f", c=C)
        rel_row = split[:, :, :].rearrange("p s f -> p (s f)")[:, 0:2 * HALF * PAIR].bitcast(i16) \
            .rearrange("p (h e) -> p h e", h=2)
        stats = sb("stats", [P, C, 6], f32)
        mean_var = sb("mean_var", [P, 2, C, 2], f32)
        std = sb("std", [P, 2, C], f32)
        rstd = sb("rstd", [P, 2, C], f32)

        ident = sb("ident", [P, P], f32)
        ones = stage[:, 6 * P:7 * P]
        zeros = sb("zeros", [P, P], bf16)
        ident_bf = sb("ident_bf", [P, P], bf16)
        iota16 = sb("iota16", [P, W], i16)
        iota_f = sb("iota_f", [P, W], f32)
        node_i = sb("node_i", [P, C], i32)
        node_c = sb("node_c", [P, C], f32)
        group_i = stage[:, 7 * P + 12 * BLOCKS:7 * P + 12 * BLOCKS + RG].bitcast(i32)
        group_c = stage[:, 7 * P + 13 * BLOCKS:7 * P + 13 * BLOCKS + RG]
        first_i = stage[:, 7 * P + 0 * BLOCKS:7 * P + 1 * BLOCKS].bitcast(i32)
        first_f = stage[:, 7 * P + 1 * BLOCKS:7 * P + 2 * BLOCKS]
        block_f = stage[:, 7 * P + 2 * BLOCKS:7 * P + 3 * BLOCKS]

        before = stage[:, 0:P]
        steps_down = sb("steps_down", [P, 1], f32)
        unordered = sb("unordered", [1, 1], i32)
        place = stage[:, 7 * P + 3 * BLOCKS:7 * P + 4 * BLOCKS]
        edge_hot = stage[:, 2 * P:2 * P + BLOCKS]
        edge_rank = stage[:, 2 * P + BLOCKS:2 * P + 2 * BLOCKS]
        edge_place = sb("edge_place", [P, 1], f32)
        edge_place_i = sb("edge_place_i", [P, 1], i32)
        edge_now = sb("edge_now", [P, 2], i32)
        last_i = stage[:, 7 * P + 5 * BLOCKS:7 * P + 5 * BLOCKS + RG].bitcast(i32)
        last_f = stage[:, 7 * P + 6 * BLOCKS:7 * P + 6 * BLOCKS + RG]
        below = stage[:, 3 * P:3 * P + RG * BLOCKS].rearrange("p (r b) -> p r b", r=RG)
        start = stage[:, 7 * P + 4 * BLOCKS:7 * P + 5 * BLOCKS]
        group_b = stage[:, 7 * P + 7 * BLOCKS:7 * P + 7 * BLOCKS + RG]
        group_b512 = stage[:, 7 * P + 11 * BLOCKS:7 * P + 11 * BLOCKS + RG]
        group_bi = stage[:, 7 * P + 9 * BLOCKS:7 * P + 9 * BLOCKS + RG].bitcast(i32)
        pair_f = stage[:, 7 * P + 8 * BLOCKS:7 * P + 8 * BLOCKS + RG]
        pair_i = stage[:, 7 * P + 10 * BLOCKS:7 * P + 10 * BLOCKS + RG].bitcast(i32)
        base_row = sb("base_row", [1, RG * P], i32)

        w1_s = sb("w1_s", [P, D], f32)
        w2_s = sb("w2_s", [P, D], f32)
        b1_s = sb("b1_s", [P, 1], f32)
        b2_s = sb("b2_s", [P, 1], f32)
        w_s = sb("w_s", [P, 2, D], f32)
        wa_s = sb("wa_s", [P, 2], f32)
        a_row = stage[:, 5 * P:5 * P + D]
        a_08 = sb("a_08", [P, D], f32)
        junk = stage[:, P:P + D]
        linear_s = sb("linear_s", [P, 2, C, 2], f32)
        ln_eps = sb("ln_eps", [P, 1], f32)
        eps1 = sb("eps1", [P, LAYERS], f32)
        score = sb("score", [P, TPI], f32)
        inside = sb("inside", [P, TPI], f32)
        rel_turn = sb("rel_turn", [P, TPI], f32)
        outside = sb("outside", [P, TPI], f32)
        masked_s = sb("masked_s", [P, TPI], f32)
        hilo_i = sb("hilo_i", [P, 2, TPI], i32)
        hilo = sb("hilo", [P, 2, TPI], f32)
        att = sb("att", [P, TPI], f32)

        ps = [ctx.enter_context(nc.psum_tensor(f"ps{i}", [P, W], f32)) for i in range(8)]
        HI = -(-N // P)
        den_ps = ps[4][:, 0:HI]

        const_in = sem("const_in")
        edges_in = sem("edges_in")
        last_in = sem("last_in")
        base_out = sem("base_out")
        base_in = sem("base_in")
        rel_out = sem("rel_out")
        given_in = sem("given_in")
        down_ready = sem("down_ready")
        down_summed = sem("down_summed")
        order_known = sem("order_known")
        starts_ready = sem("starts_ready")
        starts_summed = sem("starts_summed")
        edge_hot_ready = sem("edge_hot_ready")
        edge_ranked = sem("edge_ranked")
        edge_placed = sem("edge_placed")
        edge_moved = sem("edge_moved")
        regrouped = sem("regrouped")
        consts = sem("consts")
        ones_set = sem("ones_set")
        counted = sem("counted")
        summed_b = sem("summed_b")
        pairs_ready = sem("pairs_ready")
        edges_g = sem("edges_g")
        g_ready = sem("g_ready")
        g_flipped = sem("g_flipped")
        g_taken = sem("g_taken")
        weights_in = sem("weights_in")
        x_loaded = sems("x_loaded", 2)
        x_flipped = sem("x_flipped")
        x_taken = sem("x_taken")
        split_done = sem("split_done")
        table_out = sems("table_out", 2)
        staged = sem("staged")
        row_in = sems("row_in", TPI)
        hot_ready = sem("hot_ready")
        group_summed = sem("group_summed")
        bank_free = sem("bank_free")
        up_done = sem("up_done")
        hid_done = sem("hid_done")
        down_done = sem("down_done")
        h_done = sem("h_done")
        agg_set = sem("agg_set")
        h_flipped = sem("h_flipped")
        var_ready = sem("var_ready")
        std_ready = sem("std_ready")
        norm_done = sem("norm_done")
        x1_kept = sem("x1_kept")
        x1_flipped = sem("x1_flipped")
        x1_t_done = sem("x1_t_done")
        linear_done = sem("linear_done")
        pq_done = sem("pq_done")
        linear_taken = sem("linear_taken")
        p_taken = sem("p_taken")
        p_split = sem("p_split")
        q_taken = sem("q_taken")
        p_stored = sems("p_stored", 2)
        rel_in = sems("rel_in", 2)
        pre_ready = sem("pre_ready")
        pos_ready = sem("pos_ready")
        score_ready = sem("score_ready")
        masked = sem("masked")
        exp_ready = sem("exp_ready")
        exp_kept = sem("exp_kept")
        den_hot_ready = sem("den_hot_ready")
        den_added = sem("den_added")
        rden_kept = sem("rden_kept")
        x1_stored = sem("x1_stored")
        agg_zero = sem("agg_zero")
        sum_staged = sem("sum_staged")
        sum_flipped = sem("sum_flipped")
        y_ready = sem("y_ready")
        out_ready = sem("out_ready")
        out_stored = sems("out_stored", 2)
        passed = sem("passed")
        dve_own = sem("dve_own")
        pool_own = sem("pool_own")

        CONSTS = 10
        DEN_TILES_PE = [(), (), range(0, 3), range(3, 6), range(6, 9), range(9, 12), range(12, 14), range(14, TPI)]
        DEN_TILES_DVE = [range(0, 4), range(4, 8), range(8, 11), range(11, 14), range(14, TPI), (), (), ()]
        CREDIT = GPI
        LAST = BLOCKS - 1
        PASS_A, PASS_B = LAYERS, LAYERS + 1

        def stand_alone(eng):
            eng.sem_inc(passed, 1)

        def block_pairs(eng, body):
            with eng.Fori(0, LAST // 2) as i:
                body([(2 * i, 0, i), (2 * i + 1, 1, i)], False)
            body([(LAST, 0, LAST // 2)], True)

        def overlapped_pairs(eng, body):
            def two(i):
                return [(2 * i, 0, i), (2 * i + 1, 1, i)]

            last = [(LAST, 0, LAST // 2)]
            with eng.Fori(0, LAST // 2 - 1) as i:
                body(two(i), two(i + 1))
            body(two(LAST // 2 - 1), last)
            body(last, [])

        def pq_banks(s):
            return (ps[2 * s][:, :].rearrange("p (c d) -> p c d", c=C), ps[2 * s + 1][:, :].rearrange("p (c d) -> p c d", c=C))

        def x_rows(ap, b, tail):
            if not tail:
                return [(slice(0, P), slice(0, C), ap[ds(b * W, W), :].rearrange("(c p) d -> p c d", p=P))]
            n0 = LAST * W
            full = ap[n0:n0 + TAIL_C * P, :].rearrange("(c p) d -> p c d", p=P)
            part = ap[n0 + TAIL_C * P:N, :].rearrange("(c p) d -> p c d", c=1)
            return [(slice(0, P), slice(0, TAIL_C), full), (slice(0, TAIL_R), slice(TAIL_C, TAIL_C + 1), part)]

        def q_block(b):
            return q_rows[:, ds(b * (C * Q_SPLIT), C * Q_SPLIT)].rearrange("p (c f) -> p c f", c=C)

        def pair_sums(j):
            return ps[j % BANKS][:, 0:2 * PW].rearrange("p (k d) -> p k d", k=2)

        X_TAIL = 2

        def x_loads(stage_no, s, uses, tail):
            per = (LAST // 2 + X_TAIL, LAST // 2)[s]
            return 16 * (stage_no * per + (per if tail else uses + 1))

        def stores(stage_no, s, uses):
            return 16 * (1 + stage_no * (LAST // 2 + (s == 0)) + uses)

        block = ctx.enter_context(nc.Block())

        @block.sync
        def _(sp):
            sp.sem_inc(table_out[0], 16)
            sp.sem_inc(table_out[1], 16)
            sp.sem_inc(p_stored[0], 16)
            sp.sem_inc(p_stored[1], 16)
            sp.sem_inc(out_stored[0], 16)
            sp.sem_inc(out_stored[1], 16)
            flat = "q e -> (q e)"
            for given, ours in ((src, edge_src), (dst, edge_dst)):
                sp.dma_start(ours.rearrange(flat)[0:E].rearrange("(p e) -> p e", p=EP),
                             given.rearrange("(p e) -> p e", p=EP)).then_inc(edges_in, 16)
            sp.dma_start(given_src, src.rearrange("(p e) -> p e", p=EP)).then_inc(given_in, 16)
            sp.dma_start(given_dst[:, 0:EC], dst.rearrange("(p e) -> p e", p=EP)).then_inc(given_in, 16)
            sp.wait_ge(consts, CONSTS)
            sp.dma_start(given_dst[0:EP - 1, EC:EC + 1], dst[EC:E].rearrange("(p e) -> p e", e=EC)[:, 0:1],
                         allow_slow_non_contiguous=True).then_inc(given_in, 16)
            for ours, pad in ((edge_src, pad_src), (edge_dst, pad_dst)):
                sp.dma_start(ours.rearrange(flat)[E:QPAD].rearrange("(p e) -> p e", p=PP),
                             pad).then_inc(edges_in, 16)
            sp.dma_start(eps1[:, 0:LAYERS], eps.rearrange("(o l) -> o l", o=1).to_broadcast([P, LAYERS])).then_inc(const_in, 16)
            sp.dma_start(a_row, a.rearrange("c o -> o c").to_broadcast([P, D])).then_inc(const_in, 16)
            sp.dma_start(w_s[:, :, :], w.rearrange("(h f) c -> f h c", h=2)).then_inc(const_in, 16)
            sp.wait_ge(edges_in, 64)
            sp.wait_ge(order_known, 1)
            with sp.If(sp.value_load(unordered[0:1, 0:1], min_val=0, max_val=E) > 0):
                sp.wait_ge(regrouped, 1)
            sp.dma_start(last_i[:, :], edge_dst[:, PAIR - 1:PAIR].rearrange("(r p) o -> p (r o)", p=P),
                         allow_slow_non_contiguous=True).then_inc(last_in, 16)

            def load_x(stage_no, b, s, tail):
                for p, c, rows_of_x in x_rows(x, b, tail):
                    sp.dma_start(x_in[p, s, c, :], rows_of_x).then_inc(x_loaded[s], 16)

            def store_table(stage_no, b, s):
                sp.wait_ge(split_done, 2 + stage_no * BLOCKS + b + 1)
                sp.dma_start(table_h[ds(b * W, W), :].rearrange("(c p) f -> p c f", p=P),
                             h_parts[:, s, :, :]).then_inc(table_out[s], 16)

            def prepare(blocks, tail):
                for b, s, uses in blocks:
                    sp.wait_ge(split_done, b + 1)
                    sp.wait_ge(x_flipped, b + 1)
                    load_x(0, b, s, tail)
                for b, s, uses in blocks:
                    store_table(0, b, s)

            block_pairs(sp, prepare)

            sp.wait_ge(pairs_ready, 1)
            sp.dma_start(block_row.rearrange("o (r p) -> p (o r)", p=P), group_bi[:, :],
                         allow_slow_non_contiguous=True).then_inc(base_out, 16)
            sp.wait_ge(base_out, 16)
            sp.dma_start(base_row[:, :], block_row).then_inc(base_in, 16)
            sp.wait_ge(g_ready, 1)
            sp.dma_start(rel_rows.rearrange("(r p) e -> p r e", p=P), g_rel16).then_inc(rel_out, 16)

            def load_weights(l, ready):
                sp.wait_ge(h_flipped, ready)
                sp.dma_start(w1_s[:, :], w1[l, :, :]).then_inc(weights_in, 16)
                sp.dma_start(w2_s[:, :], w2[l, :, :]).then_inc(weights_in, 16)
                sp.dma_start(b1_s[:, :], b1[l, :].rearrange("(p o) -> p o", o=1)).then_inc(weights_in, 16)
                sp.dma_start(b2_s[:, :], b2[l, :].rearrange("(p o) -> p o", o=1)).then_inc(weights_in, 16)

            with sp.Fori(0, LAYERS - 1) as l:
                sp.wait_ge(h_flipped, 2 + l * BLOCKS)
                sp.dma_start(w1_s[:, :], w1[ds(l, 1), :, :].rearrange("o p f -> (o p) f")).then_inc(weights_in, 16)
                sp.dma_start(w2_s[:, :], w2[ds(l, 1), :, :].rearrange("o p f -> (o p) f")).then_inc(weights_in, 16)
                sp.dma_start(b1_s[:, :], b1[ds(l, 1), :].rearrange("o (p q) -> (o p) q", q=1)).then_inc(weights_in, 16)
                sp.dma_start(b2_s[:, :], b2[ds(l, 1), :].rearrange("o (p q) -> (o p) q", q=1)).then_inc(weights_in, 16)
                with sp.Fori(0, LAST // 2) as i:
                    for s in range(2):
                        store_table(l + 1, 2 * i + s, s)
                store_table(l + 1, LAST, 0)
            load_weights(LAYERS - 1, 2 + (LAYERS - 1) * BLOCKS)
            sp.wait_ge(bank_free, BANKS + LAYERS * G)

            def last_rows(blocks, following):
                for b, s, uses in following:
                    sp.wait_ge(split_done, LAYERS * BLOCKS + b + 1)
                    load_x(1, b, s, len(following) == 1)
                for b, s, uses in blocks:
                    sp.wait_ge(p_split, 2 + b + 1)
                    sp.dma_start(table_p[ds(b * W, W), :].rearrange("(c p) f -> p c f", p=P),
                                 p_parts[:, s, :, :]).then_inc(p_stored[s], 16)

            for b in range(2):
                load_x(1, b, b, False)
            overlapped_pairs(sp, last_rows)

            sp.wait_ge(rel_out, 16)
            for s in range(2):
                sp.wait_ge(p_stored[s], 16 * (1 + LAST // 2 + (s == 0)))
            with sp.Fori(0, TURNS) as i:
                for h in range(2):
                    sp.wait_ge(hot_ready, LAYERS * G + i * (GPI // 2) + (h - 1) * (HALF // 2))
                    sp.dma_start(rel_row[:, h, :], rel_rows[ds(i * GPI + h * HALF, HALF), :]
                                 .rearrange("(o g) e -> o (g e)", o=1).to_broadcast([P, HALF * PAIR])).then_inc(rel_in[h], 16)

            sp.wait_ge(rden_kept, 1)
            for k in range(2):
                c0, c1 = k * HI // 2, (k + 1) * HI // 2
                sp.dma_start(table_x1[c0 * P:c1 * P, :].rearrange("(c p) d -> p c d", p=P),
                             x1_rows[:, c0:c1, :]).then_inc(x1_stored, 16)

            def store_out(blocks, tail):
                for b, s, uses in blocks:
                    sp.wait_ge(out_ready, b + 1)
                    for p, c, rows_of_out in x_rows(out, b, tail):
                        sp.dma_start(rows_of_out, norm[p, s, c, :]).then_inc(out_stored[s], 16)

            block_pairs(sp, store_out)
            sp.wait_ge(out_stored[0], 16 * (1 + LAST // 2 + X_TAIL))
            sp.wait_ge(out_stored[1], 16 * (1 + LAST // 2))

        @block.gpsimd
        def _(pool):
            own = Count(pool, consts)
            own.add(pool.memset(ident[:, :], 0.0))
            own.add(pool.iota(iota_i, [[1, W]], base=0, channel_multiplier=0))
            own.add(pool.iota(node_i[:, :], [[P, C]], base=0, channel_multiplier=1))
            own.add(pool.iota(group_i[:, :], [[P, RG]], base=0, channel_multiplier=1))
            own.add(pool.iota(first_i[:, :], [[W, BLOCKS]], base=0, channel_multiplier=0))
            own.add(pool.memset(pad_src, 0))
            own.add(pool.memset(pad_dst, NPAD))
            own.add(pool.memset(given_dst[:, EC:EC + 1], NPAD))
            pool.wait_ge(consts, 1)
            pool.wait_ge(ones_set, 1)
            own.add(pool.affine_select(out=before, in_=ones[:, :], compare_op=ALU.is_gt, fill=0.0,
                                       base=0, pattern=[[1, P]], channel_multiplier=-1))
            own.add(pool.affine_select(out=ident[:, :], in_=ident[:, :], compare_op=ALU.not_equal, fill=1.0,
                                       base=0, pattern=[[-1, P]], channel_multiplier=1))
            assert own.k == CONSTS

            pool.wait_ge(edges_in, 64)
            pool.wait_ge(order_known, 1)
            with pool.If(pool.value_load(unordered[0:1, 0:1], min_val=0, max_val=E) > 0):
                with pool.Fori(0, EC) as t:
                    pool.wait_ge(edge_placed, t + 1)
                    stand_alone(pool)
                    for n, table in enumerate((edge_src, edge_dst)):
                        pool.indirect_dma_start(out=table.rearrange("q (e o) -> (q e) o", o=1),
                                                out_offset=bass.IndirectOffsetOnAxis(ap=edge_place_i[0:EP, 0:1], axis=0),
                                                in_=edge_now[0:EP, n:n + 1], in_offset=None).then_inc(edge_moved, 16)
                    pool.wait_ge(edge_moved, 32 * (t + 1))
                pool.sem_inc(regrouped, 1)

            pool.wait_ge(pairs_ready, 1)
            for r in range(RG):
                for table, to in ((edge_src, g_src), (edge_dst, g_dst)):
                    pool.indirect_dma_start(out=to[:, r, :], out_offset=None, in_=table,
                                            in_offset=bass.IndirectOffsetOnAxis(ap=pair_i[:, r:r + 1], axis=0)) \
                        .then_inc(edges_g, 16)

            def gather_pass(no, turn, table, to, freed, group0):
                for t in range(TPI):
                    if t % (TPI // 2) == 0:
                        pool.wait_ge(staged, 2 * (no * TURNS + turn) + t // (TPI // 2) + 1)
                    if t % 2 == 0:
                        pool.wait_ge(freed, group0 + turn * GPI + t // 2 + 1)
                        stand_alone(pool)
                    pool.indirect_dma_start(out=to(t), out_offset=None, in_=table,
                                            in_offset=bass.IndirectOffsetOnAxis(ap=idx_now[:, t:t + 1], axis=0)) \
                        .then_inc(row_in[t], 16)

            with pool.Fori(0, LAYERS) as l:
                for s in range(2):
                    pool.wait_ge(table_out[s], 16 * (1 + (l + 1) * (LAST // 2 + (s == 0))))
                stand_alone(pool)
                with pool.Fori(0, TURNS) as i:
                    gather_pass(l, i, table_h, lambda t: rows[:, t, 0:SPLIT], group_summed, l * G)

            def keep(blocks, tail):
                for b, s, uses in blocks:
                    pool.wait_ge(norm_done, b + 1)
                    pool.tensor_copy(x1_rows[:, ds(b * C, C), 0:D], norm[:, s, :, :]).then_inc(x1_kept, 1)
                for b, s, uses in blocks:
                    pool.wait_ge(p_taken, 2 + b + 1)
                    stand_alone(pool)
                    split_own.add(pool.tensor_tensor(p_f[:, s, :, :], p_f[:, s, :, :], p_parts[:, s, :, 0:PW], ALU.subtract))
                    split_own.wait()
                    stand_alone(pool)
                    split_own.add(pool.tensor_copy(p_parts[:, s, :, PW:2 * PW], p_f[:, s, :, :]))
                    split_own.wait()
                    stand_alone(pool)
                    pool.tensor_tensor(p_parts[:, s, :, 2 * PW:3 * PW], p_f[:, s, :, :], p_parts[:, s, :, PW:2 * PW],
                                       ALU.subtract).then_inc(p_split, 1)

            pool.wait_ge(g_taken, RG)
            pool.wait_ge(rel_out, 16)
            pool.memset(x1_rows[:, :, D:ROW1], 0.0).then_inc(x1_kept, 2)
            pool.sem_inc(p_split, 2)
            split_own = Count(pool, pool_own)
            with pool.Fori(0, LAST // 2) as i:
                split_own.enter(i, 4)
                keep([(2 * i, 0, i), (2 * i + 1, 1, i)], False)
                split_own.leave(LAST // 2)
            keep([(LAST, 0, LAST // 2)], True)

            for s in range(2):
                pool.wait_ge(p_stored[s], 16 * (1 + LAST // 2 + (s == 0)))
            with pool.Fori(0, TURNS) as i:
                gather_pass(PASS_A, i, table_p, lambda t: rows[:, t, 0:P_SPLIT], pre_ready, 0)

            pool.wait_ge(pre_ready, CREDIT + G)
            pool.memset(agg[:, NPAD // 2:NPAD], 0.0).then_inc(agg_zero, 1)
            pool.wait_ge(x1_stored, 32)
            with pool.Fori(0, TURNS) as i:
                gather_pass(PASS_B, i, table_x1, lambda t: rows_f[:, t, 0:ROW1], group_summed, LAYERS * G)

        @block.scalar
        def _(act):
            for free, n in ((x_taken, 2), (hid_done, 2), (h_done, 2), (x1_t_done, 2), (p_taken, 2), (linear_taken, 2),
                            (pos_ready, BANKS)):
                act.sem_inc(free, n)

            act.wait_ge(ones_set, 2)

            def first_sums(blocks, tail):
                for b, s, uses in blocks:
                    act.wait_ge(x_flipped, 2 + b + 1)
                    act.activation(agg[:, ds(b * W, W)], ps[4 + s][:, :], ACT.Copy,
                                   scale=eps1[:, 0:1]).then_inc(x_taken, 1)

            block_pairs(act, first_sums)

            def stage_turn(no, turn, freed, group0, what, halves=(0, 1)):
                for h in halves:
                    act.wait_ge(freed, group0 + turn * GPI + (h + 1) * HALF)
                    c = slice(h * TPI // 2, (h + 1) * TPI // 2)
                    for of, to in what:
                        ins = act.activation(to[:, c], of[:, ds(turn * TPI + h * (TPI // 2), TPI // 2)], ACT.Copy)
                    ins.then_inc(staged, 1)

            act.wait_ge(g_taken, RG)

            def relu(nb, s):
                act.wait_ge(up_done, nb + 1)
                act.wait_ge(down_done, nb + 1)
                act.activation(hid[:, s, :], ps[6 + s][:, :], ACT.Relu, bias=b1_s[:, :]).then_inc(hid_done, 1)

            def take_h(nb, s, bank):
                act.wait_ge(down_done, 2 + nb + 1)
                act.wait_ge(h_flipped, nb + 1)
                act.activation(h_t[:, s, :], ps[bank][:, :], ACT.Identity, bias=b2_s[:, :]).then_inc(h_done, 1)

            with act.Fori(0, LAYERS - 1) as l:
                with act.Fori(0, TURNS) as i:
                    stage_turn(l, i, group_summed, l * G, ((src_t, idx_now), (rel_t, rel_now)))
                act.wait_ge(weights_in, 64 * (l + 1))

                def mlp(blocks, tail):
                    for b, s, uses in blocks:
                        relu(l * BLOCKS + b, s)
                    for b, s, uses in blocks:
                        nb = l * BLOCKS + b
                        take_h(nb, s, 4 + s)
                        act.wait_ge(h_done, 2 + nb + 1)
                        act.activation(agg[:, ds(b * W, W)], h_t[:, s, :], ACT.Copy,
                                       scale=eps1[:, ds(l + 1, 1)]).then_inc(agg_set, 1)

                block_pairs(act, mlp)
            with act.Fori(0, TURNS) as i:
                stage_turn(LAYERS - 1, i, group_summed, (LAYERS - 1) * G, ((src_t, idx_now), (rel_t, rel_now)))
            act.wait_ge(weights_in, 64 * LAYERS)

            def deviation(b, s):
                act.wait_ge(var_ready, b + 1)
                act.activation(std[:, s, :], mean_var[:, s, :, 1], ACT.Sqrt, bias=ln_eps[:, :]).then_inc(std_ready, 1)

            def mlp_norm(blocks, following):
                n0 = (LAYERS - 1) * BLOCKS
                for b, s, uses in blocks:
                    take_h(n0 + b, s, 4)
                for b, s, uses in blocks:
                    deviation(b, s)
                for b, s, uses in blocks:
                    act.wait_ge(x1_flipped, 2 + b + 1)
                    act.wait_ge(pq_done, b + 1)
                    act.activation(x1_t[:, s, :], ps[6 + s][:, :], ACT.Copy).then_inc(x1_t_done, 1)
                for b, s, uses in following:
                    relu(n0 + b, s)
                for b, s, uses in blocks:
                    act.wait_ge(linear_done, b + 1)
                    act.wait_ge(q_taken, b + 1)
                    act.activation(linear_s[:, s, :, :], ps[5][:, 0:2 * C].rearrange("p (c h) -> p c h", h=2),
                                   ACT.Copy).then_inc(linear_taken, 1)
                for b, s, uses in blocks:
                    act.wait_ge(pq_done, 2 + b + 1)
                    act.wait_ge(linear_taken, 2 + b + 1)
                    act.wait_ge(p_stored[s], stores(0, s, uses))
                    act.wait_ge(p_split, b + 1)
                    top, bottom = pq_banks(s)
                    q = q_block(b)
                    act.activation(p_f[:, s, :, 0:D], top, ACT.Copy)
                    act.activation(p_f[:, s, :, D:PW], linear_s[:, s, :, 0:1], ACT.Copy)
                    act.activation(p_parts[:, s, :, 0:D], top, ACT.Copy)
                    act.activation(p_parts[:, s, :, D:PW], linear_s[:, s, :, 0:1], ACT.Copy)
                    act.activation(q[:, :, 0:D], bottom, ACT.Copy)
                    act.activation(q[:, :, D:PW], linear_s[:, s, :, 1:2], ACT.Copy).then_inc(p_taken, 1)

            relu((LAYERS - 1) * BLOCKS, 0)
            relu((LAYERS - 1) * BLOCKS + 1, 1)
            overlapped_pairs(act, mlp_norm)

            def exponentials(i):
                act.wait_ge(masked, i + 1)
                act.activation(exp_now[:, :], masked_s[:, :], ACT.Exp).then_inc(exp_ready, 1)
                act.wait_ge(exp_ready, i + 1)
                act.activation(exp_t[:, ds(i * TPI, TPI)], exp_now[:, :], ACT.Copy).then_inc(exp_kept, 1)

            def score_turn(i, last):
                exponentials(i)
                for j in range(GPI):
                    act.wait_ge(pre_ready, CREDIT + i * GPI + j + 1)
                    act.wait_ge(score_ready, i * GPI + j + 1)
                    act.activation(pos[:, j % BANKS, :, :], pair_sums(j)[:, :, 0:D], ACT.Relu).then_inc(pos_ready, 1)
                    if j % HALF == HALF - 1 and not last:
                        stage_turn(PASS_A, i + 1, pre_ready, 0, ((src_t, idx_now),), halves=(j // HALF,))

            stage_turn(PASS_A, 0, pre_ready, 0, ((src_t, idx_now),))
            with act.Fori(0, TURNS - 1) as i:
                score_turn(i, False)
            score_turn(TURNS - 1, True)
            exponentials(TURNS)

            act.wait_ge(exp_kept, TURNS + 1)
            act.wait_ge(rden_kept, 1)
            with act.Fori(0, TURNS) as i:
                stage_turn(PASS_B, i, group_summed, LAYERS * G, ((src_t, idx_now), (rel_t, rel_now), (exp_t[:, TPI:], exp_now)))

            act.wait_ge(bank_free, BANKS + (LAYERS + 1) * G)

            def take_sums(blocks, tail):
                for b, s, uses in blocks:
                    act.wait_ge(sum_flipped, b + 1)
                    act.activation(h_t[:, s, :], agg[:, ds(b * W, W)], ACT.Copy).then_inc(sum_staged, 1)
                for b, s, uses in blocks:
                    deviation(BLOCKS + b, s)

            block_pairs(act, take_sums)

        @block.tensor
        def _(pe):
            for free, n in ((group_summed, CREDIT), (pre_ready, CREDIT), (x_flipped, 2), (down_done, 2), (h_flipped, 2),
                            (x1_flipped, 2), (pq_done, 2), (sum_flipped, 2), (den_added, 8)):
                pe.sem_inc(free, n)
            pe.wait_ge(ones_set, 1)
            pe.wait_ge(consts, CONSTS)
            pe.wait_ge(down_ready, 1)
            pe.matmul(ps[1][:, 0:1], ones[0:EP, :], steps_down[0:EP, :], start=True, stop=True).then_inc(down_summed, 1)
            pe.wait_ge(order_known, 1)
            with pe.If(pe.value_load(unordered[0:1, 0:1], min_val=0, max_val=E) > 0):
                pe.wait_ge(starts_ready, 1)
                pe.matmul(ps[0][0:EP, 0:BLOCKS], ones[0:EP, 0:EP], place[0:EP, :], start=True, stop=True).then_inc(starts_summed, 1)
                with pe.Fori(0, EC) as t:
                    pe.wait_ge(edge_hot_ready, t + 1)
                    pe.matmul(ps[1][0:EP, 0:BLOCKS], before[0:EP, 0:EP], edge_hot[0:EP, :], start=True, stop=True)
                    pe.matmul(ps[2][0:EP, 0:BLOCKS], ones[0:EP, 0:EP], edge_hot[0:EP, :], start=True, stop=True) \
                        .then_inc(edge_ranked, 1)

            pe.wait_ge(counted, 1)
            pe.matmul(ps[0][:, 0:RG * BLOCKS], ones[:, :], below[:, :, :].rearrange("p r b -> p (r b)"),
                      start=True, stop=True).then_inc(summed_b, 1)

            def flip(bank, rows_in):
                for c in range(C):
                    ins = pe.transpose(ps[bank][:, c * P:(c + 1) * P], rows_in(c), ident[:, :])
                return ins

            def flip_x(blocks, tail):
                for b, s, uses in blocks:
                    pe.wait_ge(x_loaded[s], x_loads(0, s, uses, tail))
                    pe.wait_ge(x_taken, b + 1)
                    flip(4 + s, lambda c: x_in[:, s, c, :]).then_inc(x_flipped, 1)

            block_pairs(pe, flip_x)

            pe.wait_ge(g_ready, 1)
            for r in range(RG):
                if r >= BANKS:
                    pe.wait_ge(g_taken, r - BANKS + 1)
                for n, of in enumerate((g_srcf, g_rel)):
                    for k in range(2):
                        m = 2 * n + k
                        ins = pe.transpose(ps[r % BANKS][:, m * P:(m + 1) * P], of[:, r, k * P:(k + 1) * P], ident[:, :])
                ins.then_inc(g_flipped, 1)
            pe.wait_ge(g_taken, RG)

            def sum_turn(turn_all, group0, turn, hot0, product):
                for j in range(GPI):
                    g = group0 + turn * GPI + j
                    pe.wait_ge(bank_free, g + 1)
                    pe.wait_ge(hot_ready, hot0 + turn * GPI + j + 1)
                    for k in range(2):
                        pe.wait_ge(row_in[2 * j + k], 16 * (turn_all + 1))
                        ins = product(j, k)
                    ins.then_inc(group_summed, 1)

            def product_h(j, k):
                for part in range(3):
                    ins = pe.matmul(ps[j % BANKS][:, :], rows[:, 2 * j + k, part * D:(part + 1) * D], hot_bf[:, j % BANKS, k, :],
                                    start=(k == 0 and part == 0), stop=(k == 1 and part == 2))
                return ins

            def product_x1(j, k):
                return pe.matmul(ps[j % BANKS][:, :], rows_f[:, 2 * j + k, 0:D], hot_w[:, j % BANKS, k, :],
                                 start=(k == 0), stop=(k == 1))

            def layer_sums(l):
                with pe.Fori(0, TURNS) as i:
                    sum_turn(l * TURNS + i, l * G, i, l * G, product_h)
                pe.wait_ge(bank_free, BANKS + (l + 1) * G)
                pe.wait_ge(weights_in, 64 * (l + 1))
                stand_alone(pe)

            def up(nb, b, s):
                pe.wait_ge(hid_done, nb + 1)
                pe.matmul(ps[6 + s][:, :], w1_s[:, :], agg[:, ds(b * W, W)], start=True, stop=True).then_inc(up_done, 1)

            def down(nb, s, bank, free):
                pe.wait_ge(hid_done, 2 + nb + 1)
                pe.wait_ge(h_done, nb + 1 + free)
                pe.matmul(ps[bank][:, :], w2_s[:, :], hid[:, s, :], start=True, stop=True).then_inc(down_done, 1)

            def flip_h(nb, s):
                pe.wait_ge(h_done, 2 + nb + 1)
                pe.wait_ge(split_done, BLOCKS + nb + 1)
                flip(2 + s, lambda c: h_t[:, s, c * P:(c + 1) * P]).then_inc(h_flipped, 1)

            with pe.Fori(0, LAYERS - 1) as l:
                layer_sums(l)

                def mlp(blocks, tail):
                    for b, s, uses in blocks:
                        up(l * BLOCKS + b, b, s)
                    for b, s, uses in blocks:
                        down(l * BLOCKS + b, s, 4 + s, 0)
                    for b, s, uses in blocks:
                        flip_h(l * BLOCKS + b, s)

                block_pairs(pe, mlp)
                pe.wait_ge(split_done, 2 + (l + 2) * BLOCKS)
                stand_alone(pe)
            layer_sums(LAYERS - 1)

            n0 = (LAYERS - 1) * BLOCKS

            def up_norm(b, s):
                pe.wait_ge(x1_t_done, b + 1)
                up(n0 + b, b, s)

            def mlp_norm(blocks, following):
                for b, s, uses in blocks:
                    down(n0 + b, s, 4, 1)
                for b, s, uses in blocks:
                    pe.wait_ge(p_taken, 2 + b - s)
                    pe.wait_ge(q_taken, 2 + b - s)
                    flip_h(n0 + b, s)
                for b, s, uses in blocks:
                    pe.wait_ge(norm_done, b + 1)
                    flip(6 + s, lambda c: norm[:, s, c, :]).then_inc(x1_flipped, 1)
                for b, s, uses in following:
                    up_norm(b, s)
                for b, s, uses in blocks:
                    pe.wait_ge(x1_t_done, 2 + b + 1)
                    top, bottom = pq_banks(s)
                    pe.wait_ge(linear_taken, 1 + b + 1)
                    chunks = [x1_t[:, s, c * P:(c + 1) * P] for c in range(C)]
                    for c in range(C):
                        ins = pe.matmul(ps[5][:, 2 * c:2 * c + 2], chunks[c], wa_s[:, :], start=True, stop=True)
                    ins.then_inc(linear_done, 1)
                    for c in range(C):
                        pe.matmul(top[:, c, :], chunks[c], w_s[:, 0, :], start=True, stop=True)
                        ins = pe.matmul(bottom[:, c, :], chunks[c], w_s[:, 1, :], start=True, stop=True)
                    ins.then_inc(pq_done, 1)

            up_norm(0, 0)
            up_norm(1, 1)
            overlapped_pairs(pe, mlp_norm)
            pe.wait_ge(p_taken, 2 + BLOCKS)
            pe.wait_ge(q_taken, 2 + BLOCKS)

            def add_den(t, n, last=False):
                pe.wait_ge(den_hot_ready, n + 1)
                pe.matmul(den_ps, den_hot[:, t % 8, 1, :], den_hot[:, t % 8, 0, 0:HI],
                          start=False, stop=False).then_inc(den_added, 1)

            pe.matmul(den_ps, zeros[:, :], zeros[:, 0:HI], start=True, stop=False)
            with pe.Fori(0, TURNS) as i:
                _, blocks_now = nc.values_load_multi_w_load_instructions(
                    base_row[0:1, ds(i * GPI, GPI)], engines=(mybir.EngineType.PE,), min_val=0, max_val=LAST,
                    skip_runtime_bounds_check_because="a group's block, by its making")
                for j in range(GPI):
                    g = i * GPI + j
                    pe.wait_ge(score_ready, g + 1)
                    if j % 2 == 0:
                        pe.wait_ge(hot_ready, LAYERS * G + i * (GPI // 2) + j // 2 + 1)
                    q0 = blocks_now[j] * (C * Q_SPLIT)
                    for k in range(2):
                        of_tile = slice((j % 2) * PAIR + k * P, (j % 2) * PAIR + (k + 1) * P)
                        for c in range(C):
                            for part in range(3):
                                pe.matmul(pair_sums(j)[:, k, :], hot_t[:, j // 2, c, of_tile],
                                          q_rows[:, ds(q0 + c * Q_SPLIT + part * Q_PART, PW)],
                                          start=(c == 0 and part == 0), stop=False)
                        pe.wait_ge(row_in[2 * j + k], 16 * (PASS_A * TURNS + i + 1))
                        for part in range(3):
                            ins = pe.matmul(pair_sums(j)[:, k, :], ident_bf[:, :], rows[:, 2 * j + k, part * PW:(part + 1) * PW],
                                            start=False, stop=(part == 2))
                    ins.then_inc(pre_ready, 1)
                    for t in DEN_TILES_PE[j]:
                        add_den(t, i * TPI + t)
            for t in range(TPI):
                add_den(t, TURNS * TPI + t)
            pe.matmul(den_ps, zeros[:, :], zeros[:, 0:HI], start=False, stop=True).then_inc(den_added, 1)

            with pe.Fori(0, TURNS) as i:
                sum_turn(PASS_B * TURNS + i, LAYERS * G, i, LAYERS * G + G // 2, product_x1)
            pe.wait_ge(bank_free, BANKS + (LAYERS + 1) * G)

            def flip_sums(blocks, tail):
                for b, s, uses in blocks:
                    pe.wait_ge(sum_staged, b + 1)
                    pe.wait_ge(y_ready, b + 1)
                    flip(2 + s, lambda c: h_t[:, s, c * P:(c + 1) * P]).then_inc(sum_flipped, 1)

            block_pairs(pe, flip_sums)

        @block.vector
        def _(dve):
            own = Count(dve, dve_own)
            for free, n in ((bank_free, BANKS), (split_done, 2), (q_taken, 2), (y_ready, 2), (score_ready, BANKS)):
                dve.sem_inc(free, n)
            dve.memset(zeros[:, :], 0.0)
            dve.memset(hilo[:, :, :], 0.0)
            dve.memset(score[:, :], 0.0)
            dve.memset(inside[:, :], 0.0)
            dve.memset(outside[:, :], -1e30)
            dve.memset(ln_eps[:, :], LN_EPS)
            dve.memset(ones[:, :], 1.0).then_inc(ones_set, 1)
            dve.wait_ge(consts, CONSTS)
            dve.tensor_copy(iota_f[:, :], iota_i)
            dve.tensor_copy(ident_bf[:, :], ident[:, :])
            dve.tensor_copy(iota16[:, :], iota_i)
            dve.tensor_copy(node_c[:, :], node_i[:, :])
            dve.tensor_copy(group_c[:, :], group_i[:, :])
            own.add(dve.tensor_copy(first_f[:, :], first_i[:, :]))
            own.wait()
            own.add(dve.tensor_scalar(block_f[:, :], first_f[:, :], 1.0 / W, None, ALU.mult))
            dve.wait_ge(given_in, 48)
            own.add(dve.tensor_single_scalar(given_bi, given_dst, W.bit_length() - 1, ALU.logical_shift_right))
            own.wait()
            own.add(dve.tensor_copy(given_b, given_bi))
            own.wait()
            own.add(dve.tensor_tensor(given_down, given_b[:, 1:EC + 1], given_b[:, 0:EC], ALU.is_lt))
            own.wait()
            dve.reduce_sum(steps_down[0:EP, :], given_down, axis=AX).then_inc(down_ready, 1)
            dve.wait_ge(down_summed, 1)
            dve.tensor_copy(unordered[:, :], ps[1][0:1, 0:1]).then_inc(order_known, 1)
            dve.wait_ge(order_known, 1)
            with dve.If(dve.value_load(unordered[0:1, 0:1], min_val=0, max_val=E) > 0):
                own_before = (own.base, own.k)
                for b in range(BLOCKS):
                    own.add(dve.tensor_scalar(given_down, given_b[:, 0:EC], float(b), 0.0, ALU.is_lt, ALU.add,
                                              accum_out=place[0:EP, b:b + 1]))
                    own.wait()
                dve.sem_inc(starts_ready, 1)
                dve.wait_ge(starts_summed, 1)
                own.add(dve.tensor_copy(place[0:EP, :], ps[0][0:EP, 0:BLOCKS]))
                own.wait()
                with dve.Fori(0, EC) as t:
                    own.enter(t, 6)
                    own.wait()
                    dve.tensor_scalar(edge_hot[0:EP, :], block_f[0:EP, :], given_b[:, ds(t, 1)], None, ALU.is_equal) \
                        .then_inc(edge_hot_ready, 1)
                    own.add(dve.tensor_copy(edge_now[0:EP, 0:1], given_src[:, ds(t, 1)]))
                    own.add(dve.tensor_copy(edge_now[0:EP, 1:2], given_dst[:, ds(t, 1)]))
                    dve.wait_ge(edge_ranked, t + 1)
                    own.add(dve.tensor_tensor(edge_rank[0:EP, :], ps[1][0:EP, 0:BLOCKS], place[0:EP, :], ALU.add))
                    own.wait()
                    own.add(dve.tensor_tensor(place[0:EP, :], ps[2][0:EP, 0:BLOCKS], place[0:EP, :], ALU.add))
                    own.add(dve.tensor_tensor(edge_rank[0:EP, :], edge_rank[0:EP, :], edge_hot[0:EP, :], ALU.mult))
                    own.wait()
                    own.add(dve.reduce_sum(edge_place[0:EP, :], edge_rank[0:EP, :], axis=AX))
                    own.wait()
                    dve.tensor_copy(edge_place_i[0:EP, :], edge_place[0:EP, :]).then_inc(edge_placed, 1)
                    dve.wait_ge(edge_moved, 32 * (t + 1))
                    own.leave(EC)
                regroup_adds = own.base + own.k - sum(own_before)
            with dve.Else():
                dve.sem_inc(dve_own, regroup_adds)
            dve.wait_ge(const_in, 48)
            for h in range(2):
                own.add(dve.tensor_tensor_reduce(out=junk, in0=w_s[:, h, :], in1=a_row, scale=NEG_SLOPE, scalar=0.0,
                                                 op0=ALU.mult, op1=ALU.add, accum_out=wa_s[:, h:h + 1]))
                own.wait()
            dve.tensor_scalar(a_08[:, :], a_row, 1.0 - NEG_SLOPE, None, ALU.mult)
            dve.tensor_scalar(eps1[:, :], eps1[:, :], 1.0, None, ALU.add).then_inc(ones_set, 1)

            dve.wait_ge(last_in, 16)
            own.add(dve.tensor_copy(last_f[:, :], last_i[:, :]))
            own.wait()
            for r in range(RG):
                ins = dve.tensor_scalar(below[:, r, :], first_f[:, :], last_f[:, r:r + 1], None, ALU.is_gt)
            ins.then_inc(counted, 1)
            dve.wait_ge(summed_b, 1)
            own.add(dve.tensor_reduce(start[:, :], ps[0][:, 0:RG * BLOCKS].rearrange("p (r b) -> p b r", r=RG), axis=AX, op=ALU.add))
            own.wait()
            own.add(dve.tensor_tensor(start[:, :], start[:, :], block_f[:, :], ALU.add))
            own.wait()
            for r in range(RG):
                own.add(dve.tensor_scalar(junk[:, 0:LAST], start[:, 1:BLOCKS], group_c[:, r:r + 1], 0.0, ALU.is_le, ALU.add,
                                          accum_out=group_b[:, r:r + 1]))
                own.wait()
            dve.tensor_copy(group_bi[:, :], group_b[:, :])
            dve.tensor_scalar(group_b512[:, :], group_b[:, :], float(W), None, ALU.mult)
            own.add(dve.tensor_tensor(pair_f[:, :], group_c[:, :], group_b[:, :], ALU.subtract))
            own.wait()
            dve.tensor_copy(pair_i[:, :], pair_f[:, :]).then_inc(pairs_ready, 1)

            def split_rows(u, of, s, uses):
                dve.wait_ge(table_out[s], stores(u, s, uses))
                own.add(dve.tensor_copy(h_parts[:, s, :, 0:D], of))
                own.wait()
                own.add(dve.tensor_tensor(rest[:, :, 0:D], of, h_parts[:, s, :, 0:D], ALU.subtract))
                own.wait()
                own.add(dve.tensor_copy(h_parts[:, s, :, D:2 * D], rest[:, :, 0:D]))
                own.wait()
                dve.tensor_tensor(h_parts[:, s, :, 2 * D:3 * D], rest[:, :, 0:D], h_parts[:, s, :, D:2 * D],
                                  ALU.subtract).then_inc(split_done, 1)

            with dve.Fori(0, LAST // 2) as i:
                own.enter(i, 6)
                for s in range(2):
                    dve.wait_ge(x_loaded[s], x_loads(0, s, i, False))
                    split_rows(0, x_in[:, s, :, :], s, i)
                own.leave(LAST // 2)
            dve.wait_ge(x_loaded[0], x_loads(0, 0, LAST // 2, True))
            split_rows(0, x_in[:, 0, :, :], 0, LAST // 2)

            dve.wait_ge(edges_g, 16 * 2 * RG)
            dve.tensor_copy(g_srcf, g_src)
            for r in range(RG):
                ins = dve.tensor_scalar(g_rel[:, r, :], g_dst[:, r, :], group_b512[:, r:r + 1], None, ALU.subtract)
            own.add(ins)
            own.wait()
            dve.tensor_copy(g_rel16, g_rel).then_inc(g_ready, 1)
            for r in range(RG):
                n = min(P, G - r * P)
                dve.wait_ge(g_flipped, r + 1)
                for m, to in ((0, src_t), (1, rel_t)):
                    ins = dve.tensor_copy(to[:, 2 * r * P:2 * (r * P + n)].rearrange("p (g k) -> p k g", k=2),
                                          ps[r % BANKS][:, m * PAIR:(m + 1) * PAIR].rearrange("p (k g) -> p k g", k=2)[:, :, 0:n])
                ins.then_inc(g_taken, 1)
            dve.wait_ge(base_in, 16)

            def load_blocks(turn):
                _, values = nc.values_load_multi_w_load_instructions(
                    base_row[0:1, ds(turn * GPI, GPI)], engines=(mybir.EngineType.DVE,), min_val=0, max_val=LAST,
                    skip_runtime_bounds_check_because="a group's block, by its making")
                return values

            def add_group(g, j, b):
                dve.wait_ge(group_summed, CREDIT + g + 1)
                dve.wait_ge(bank_free, BANKS + g)
                sums = agg[:, ds(b * W, W)]
                dve.tensor_tensor(sums, sums, ps[j % BANKS][:, :], ALU.add).then_inc(bank_free, 1)

            def sum_turn(pass_no, group0, turn, one_hot):
                b = load_blocks(turn)
                for j in range(GPI):
                    if j % HALF == 0:
                        dve.wait_ge(staged, 2 * (pass_no * TURNS + turn) + j // HALF + 1)
                    dve.wait_ge(group_summed, group0 + turn * GPI + j + 1 + CREDIT - BANKS)
                    one_hot(j)
                    if j >= 2:
                        add_group(group0 + turn * GPI + j - 2, j - 2, b[j - 2])
                for j in (GPI - 2, GPI - 1):
                    add_group(group0 + turn * GPI + j, j, b[j])

            def hot_h(j):
                for k in range(2):
                    ins = dve.tensor_scalar(hot_bf[:, j % BANKS, k, :], iota16[:, :], rel_now[:, 2 * j + k:2 * j + k + 1],
                                            None, ALU.is_equal)
                ins.then_inc(hot_ready, 1)

            def layer_sums(l):
                dve.wait_ge(x_taken, 2 + BLOCKS)
                dve.wait_ge(split_done, 2 + (l + 1) * BLOCKS)
                stand_alone(dve)
                with dve.Fori(0, TURNS) as i:
                    sum_turn(l, l * G, i, hot_h)

            with dve.Fori(0, LAYERS - 1) as l:
                layer_sums(l)
                own.enter(l, 3 * BLOCKS)
                with dve.Fori(0, LAST // 2) as i:
                    own.enter(i, 6)
                    for s in range(2):
                        dve.wait_ge(h_flipped, 2 + l * BLOCKS + 2 * i + s + 1)
                        split_rows(l + 1, ps[2 + s][:, :].rearrange("p (c d) -> p c d", c=C), s, i)
                    own.leave(LAST // 2)
                dve.wait_ge(h_flipped, 2 + l * BLOCKS + BLOCKS)
                split_rows(l + 1, ps[2][:, :].rearrange("p (c d) -> p c d", c=C), 0, LAST // 2)
                dve.wait_ge(agg_set, (l + 1) * BLOCKS)
                own.leave(LAYERS - 1)
            layer_sums(LAYERS - 1)

            def moments(s, done, value):
                dve.wait_ge(done, value)
                for c in range(C):
                    ins = dve.bn_stats(stats[:, c, :], y[:, s, c, :])
                own.add(ins)
                own.wait()
                stand_alone(dve)
                for c in range(C):
                    ins = dve.bn_aggr(mean_var[:, s, c, :], stats[:, c, :])
                ins.then_inc(var_ready, 1)

            def normalise(b, s):
                dve.wait_ge(var_ready, b + 1)
                dve.wait_ge(std_ready, b + 1)
                own.add(dve.reciprocal(rstd[:, s, :], std[:, s, :]))
                own.wait()
                for c in range(C):
                    ins = dve.tensor_scalar(norm[:, s, c, :], y[:, s, c, :], mean_var[:, s, c, 0:1], rstd[:, s, c:c + 1],
                                            ALU.subtract, ALU.mult)
                return ins

            def x1_blocks(blocks, tail):
                n0 = (LAYERS - 1) * BLOCKS
                for b, s, uses in blocks:
                    dve.wait_ge(x_loaded[s], x_loads(1, s, uses, tail))
                    dve.wait_ge(h_flipped, 2 + n0 + b + 1)
                    dve.tensor_tensor(y[:, s, :, :], ps[2 + s][:, :].rearrange("p (c d) -> p c d", c=C), x_in[:, s, :, :],
                                      ALU.add).then_inc(split_done, 1)
                    moments(s, split_done, 2 + LAYERS * BLOCKS + b + 1)
                for b, s, uses in blocks:
                    dve.wait_ge(x1_flipped, b + 1)
                    dve.wait_ge(x1_kept, b + 1)
                    normalise(b, s).then_inc(norm_done, 1)
                for b, s, uses in blocks:
                    dve.wait_ge(p_taken, 2 + b + 1)
                    dve.wait_ge(q_taken, 2 + b)
                    q = q_block(b)
                    top, bottom = pq_banks(s)
                    dve.tensor_tensor(rest[:, :, 0:D], bottom, q[:, :, 0:D], ALU.subtract)
                    own.add(dve.tensor_tensor(rest[:, :, D:PW], linear_s[:, s, :, 1:2], q[:, :, D:PW], ALU.subtract))
                    own.wait()
                    own.add(dve.tensor_copy(q[:, :, Q_PART:Q_PART + PW], rest[:, :, 0:PW]))
                    own.wait()
                    dve.tensor_tensor(q[:, :, 2 * Q_PART:2 * Q_PART + PW], rest[:, :, 0:PW], q[:, :, Q_PART:Q_PART + PW],
                                      ALU.subtract).then_inc(q_taken, 1)

            with dve.Fori(0, LAST // 2) as i:
                own.enter(i, 8)
                x1_blocks([(2 * i, 0, i), (2 * i + 1, 1, i)], False)
                own.leave(LAST // 2)
            x1_blocks([(LAST, 0, LAST // 2)], True)

            def den_tile(t, n):
                dve.wait_ge(den_added, n + 1)
                dve.tensor_scalar(den_hot[:, t % 8, 0, 0:HI], iota_f[:, 0:HI], hilo[:, 0, t:t + 1], exp_now[:, t:t + 1],
                                  ALU.is_equal, ALU.mult)
                dve.tensor_scalar(den_hot[:, t % 8, 1, :], iota_f[:, 0:P], hilo[:, 1, t:t + 1], None,
                                  ALU.is_equal).then_inc(den_hot_ready, 1)

            def scores(i, j):
                dve.wait_ge(pos_ready, BANKS + i * GPI + j + 1)
                for k in range(2):
                    ins = dve.tensor_tensor_reduce(out=pos[:, j % BANKS, k, :], in0=pos[:, j % BANKS, k, :], in1=a_08[:, :], scale=1.0,
                                                   scalar=pair_sums(j)[:, k, D:PW], op0=ALU.mult, op1=ALU.add,
                                                   accum_out=score[:, 2 * j + k:2 * j + k + 1])
                ins.then_inc(score_ready, 1)

            def mask_scores(i):
                dve.wait_ge(score_ready, BANKS + i * GPI)
                own.add(dve.tensor_tensor(score[:, :], score[:, :], inside[:, :], ALU.mult))
                own.wait()
                dve.tensor_tensor(masked_s[:, :], score[:, :], outside[:, :], ALU.add).then_inc(masked, 1)

            def hot_pairs(i, d):
                if d % 2 == 0:
                    dve.wait_ge(rel_in[d // 2], 16 * (i + 1))
                dve.wait_ge(pre_ready, i * GPI + 2 * d + 2)
                for c in range(C):
                    ins = dve.tensor_scalar(hot_t[:, d, c, :], rel_row[:, d // 2, (d % 2) * 2 * PAIR:(d % 2 + 1) * 2 * PAIR],
                                            node_c[:, c:c + 1], None, ALU.is_equal)
                ins.then_inc(hot_ready, 1)

            def score_turn(i, last):
                mask_scores(i)
                hot_pairs(i, 2)
                hot_pairs(i, 3)
                for j in range(GPI):
                    scores(i, j)
                    if DEN_TILES_DVE[j]:
                        dve.wait_ge(exp_ready, i + 1)
                    for t in DEN_TILES_DVE[j]:
                        den_tile(t, i * TPI + t)
                    if j == HALF:
                        dve.tensor_single_scalar(hilo_i[:, 0, :], src_t[:, ds(i * TPI, TPI)], 7, ALU.logical_shift_right)
                        own.add(dve.tensor_single_scalar(hilo_i[:, 1, :], src_t[:, ds(i * TPI, TPI)], P - 1, ALU.bitwise_and))
                        own.add(dve.tensor_copy(rel_turn[:, :], rel_t[:, ds(i * TPI, TPI)]))
                        own.wait()
                        dve.tensor_copy(hilo[:, :, :], hilo_i[:, :, :])
                        own.add(dve.tensor_scalar(inside[:, :], rel_turn[:, :], 0.0, None, ALU.is_ge))
                        own.wait()
                        own.add(dve.scalar_tensor_tensor(inside[:, :], rel_turn[:, :], float(W), inside[:, :], ALU.is_lt, ALU.mult))
                        own.wait()
                        own.add(dve.tensor_scalar(outside[:, :], inside[:, :], 1e30, -1e30, ALU.mult, ALU.add))
                    if j > HALF and j < GPI - 1 and not last:
                        hot_pairs(i + 1, j - HALF - 1)

            dve.wait_ge(x1_kept, 2 + BLOCKS)
            hot_pairs(0, 0)
            hot_pairs(0, 1)
            with dve.Fori(0, TURNS - 1) as i:
                own.enter(i, 6)
                score_turn(i, False)
                own.leave(TURNS - 1)
            score_turn(TURNS - 1, True)
            mask_scores(TURNS)
            dve.wait_ge(exp_ready, TURNS + 1)
            for t in range(TPI):
                den_tile(t, TURNS * TPI + t)
            dve.wait_ge(den_added, 8 + (TURNS + 1) * TPI + 1)
            own.add(dve.tensor_scalar(den_s[:, 0:HI], den_ps, float(np.finfo(np.float32).tiny), None, ALU.max))
            own.wait()
            dve.reciprocal(x1_rows[:, 0:HI, D], den_s[:, 0:HI]).then_inc(rden_kept, 1)
            dve.wait_ge(pre_ready, CREDIT + G)
            own.add(dve.memset(agg[:, 0:NPAD // 2], 0.0))
            own.wait()
            dve.wait_ge(agg_zero, 1)

            with dve.Fori(0, TURNS) as i:
                own.enter(i, GPI)

                def hot_x1(j):
                    for k in range(2):
                        dve.wait_ge(row_in[2 * j + k], 16 * (PASS_B * TURNS + i + 1))
                    own.add(dve.tensor_tensor(att[:, 2 * j:2 * j + 2], rows_f[:, 2 * j:2 * j + 2, D], exp_now[:, 2 * j:2 * j + 2], ALU.mult))
                    own.wait()
                    for k in range(2):
                        t = 2 * j + k
                        ins = dve.tensor_scalar(hot_w[:, j % BANKS, k, :], iota_f[:, :], rel_now[:, t:t + 1], att[:, t:t + 1],
                                                ALU.is_equal, ALU.mult)
                    ins.then_inc(hot_ready, 1)

                sum_turn(PASS_B, LAYERS * G, i, hot_x1)
                own.leave(TURNS)

            def out_blocks(blocks, tail):
                for b, s, uses in blocks:
                    dve.wait_ge(sum_flipped, 2 + b + 1)
                    dve.tensor_tensor(y[:, s, :, :], ps[2 + s][:, :].rearrange("p (c d) -> p c d", c=C),
                                      x1_rows[:, ds(b * C, C), 0:D], ALU.add).then_inc(y_ready, 1)
                    moments(s, y_ready, 2 + b + 1)
                for b, s, uses in blocks:
                    dve.wait_ge(out_stored[s], stores(0, s, uses))
                    normalise(BLOCKS + b, s).then_inc(out_ready, 1)

            with dve.Fori(0, LAST // 2) as i:
                own.enter(i, 4)
                out_blocks([(2 * i, 0, i), (2 * i + 1, 1, i)], False)
                own.leave(LAST // 2)
            out_blocks([(LAST, 0, LAST // 2)], True)


_INS = ["x", "src", "dst", "L0_gnn_W1", "L0_gnn_b1", "L0_gnn_W2", "L0_gnn_b2", "L0_gnn_eps", "L1_gnn_w", "L1_gnn_a"]


def kernel(**inputs):
    import concourse.bacc as bacc
    from concourse.bass_utils import run_bass_kernel_spmd

    nc = bacc.Bacc("TRN2", target_bir_lowering=False, num_devices=1)
    arrays, args = {}, []
    for name in _INS:
        given = np.ascontiguousarray(inputs[name])
        arrays[f"in_{name}"] = given
        args.append(nc.dram_tensor(f"in_{name}", given.shape, mybir.dt.from_np(given.dtype), kind="ExternalInput").ap())
    out = nc.dram_tensor("out", (N, D), f32, kind="ExternalOutput").ap()
    gnn(nc, *args, out)
    return run_bass_kernel_spmd(nc, [arrays], core_ids=[0]).results[0]["out"]
```
